# Optimizing a Trainium2 kernel written in Bass

```python
import numpy as np
import jax
import jax.numpy as jnp

def _softmax(x, axis=-1):
    return jax.nn.softmax(x, axis=axis)

def _gelu(x):
    return jax.nn.gelu(x, approximate=True)

def _silu(x):
    return jax.nn.silu(x)

def _sigmoid(x):
    return jax.nn.sigmoid(x)

def _layernorm(x, axis=-1, eps=1e-05):
    m = jnp.mean(x, axis=axis, keepdims=True)
    v = jnp.var(x, axis=axis, keepdims=True)
    return (x - m) / jnp.sqrt(v + eps)

def _scatter_add(tgt, idx, src, axis=0):
    return tgt.at[idx].add(src)

def _segment_sum(src, seg, n):
    return jax.ops.segment_sum(src, seg, n)
kernel_name = 'mk_gnn_preln_d1_gnn_r8_6326d7'

def setup_inputs(seed: int=0):
    np.random.seed(seed)
    _w = jnp.asarray

    def _rec_inputs():
        import jax
        import jax.numpy as jnp
        _gk = jax.random.key(seed)
        x = -0.0004942 + 1 * jax.random.normal(jax.random.fold_in(_gk, 1), (12500, 128), jnp.float32)
        _s = jax.random.randint(jax.random.fold_in(_gk, 2), (100000,), 0, 12500, jnp.int32)
        _d = jax.random.randint(jax.random.fold_in(_gk, 3), (100000,), 0, 12500, jnp.int32)
        _loop = jnp.arange(12500, dtype=jnp.int32)
        src = jnp.concatenate([_s, _d, _loop])
        dst = jnp.concatenate([_d, _s, _loop])
        _o = jnp.argsort(dst, stable=True)
        src = src[_o]
        dst = dst[_o]
        edge_type_32 = jax.random.randint(jax.random.fold_in(_gk, 12), (212500,), 0, 32, jnp.int32)
        return (x, src, dst, edge_type_32)
    x, src, dst, edge_type_32 = _rec_inputs()

    def _L0_gnn_setup():
        import jax, jax.numpy as jnp
        import numpy as np
        N = 3750
        E = 120000
        DIN = 128
        DOUT = 128
        R = 32
        NUM_RULES = 100
        ACTIVE = 4
        EPS = 1e-05
        key = jax.random.key(seed)
        ks = jax.random.split(key, 10)
        x = jax.random.normal(ks[0], (N, DIN), jnp.float32)
        src = jax.random.randint(ks[1], (E,), 0, N)
        dst = jax.random.randint(ks[2], (E,), 0, N)
        edge_type = jax.random.randint(ks[3], (E,), 0, R)
        rule_ids = jax.random.randint(ks[4], (ACTIVE,), 0, NUM_RULES)
        W_r = jax.random.normal(ks[5], (R, DIN, DOUT), jnp.float32) * 0.05
        Wq_w = jax.random.normal(ks[6], (DIN, DOUT), jnp.float32) * 0.05
        Wq_b = jnp.zeros((DOUT,), jnp.float32)
        Wk_w = jax.random.normal(ks[7], (3 * DIN, DOUT), jnp.float32) * 0.05
        Wk_b = jnp.zeros((DOUT,), jnp.float32)
        rule_emb = jax.random.normal(ks[8], (NUM_RULES, DIN), jnp.float32) * 0.05
        bias = jnp.zeros((DOUT,), jnp.float32)
        ln_gamma = jnp.ones((DOUT,), jnp.float32)
        ln_beta = jnp.zeros((DOUT,), jnp.float32)
        return {'x': x, 'W_r': W_r, 'Wq_w': Wq_w, 'Wq_b': Wq_b, 'Wk_w': Wk_w, 'Wk_b': Wk_b, 'rule_emb': rule_emb, 'bias': bias, 'ln_gamma': ln_gamma, 'ln_beta': ln_beta, 'src': src, 'dst': dst, 'edge_type': edge_type, 'rule_ids': rule_ids}
    _L0_gnn_all = _L0_gnn_setup()
    _L0_gnn_in = {k: v for k, v in _L0_gnn_all.items() if k in ('W_r', 'Wq_w', 'Wq_b', 'Wk_w', 'Wk_b', 'rule_emb', 'bias', 'ln_gamma', 'ln_beta', 'rule_ids')}
    del _L0_gnn_all
    return {'x': x, 'src': src, 'dst': dst, 'edge_type_32': edge_type_32, 'L0_gnn_W_r': _L0_gnn_in['W_r'], 'L0_gnn_Wq_w': _L0_gnn_in['Wq_w'], 'L0_gnn_Wq_b': _L0_gnn_in['Wq_b'], 'L0_gnn_Wk_w': _L0_gnn_in['Wk_w'], 'L0_gnn_Wk_b': _L0_gnn_in['Wk_b'], 'L0_gnn_rule_emb': _L0_gnn_in['rule_emb'], 'L0_gnn_bias': _L0_gnn_in['bias'], 'L0_gnn_ln_gamma': _L0_gnn_in['ln_gamma'], 'L0_gnn_ln_beta': _L0_gnn_in['ln_beta'], 'L0_gnn_rule_ids': _L0_gnn_in['rule_ids']}

def reference(x, src, dst, edge_type_32, L0_gnn_W_r, L0_gnn_Wq_w, L0_gnn_Wq_b, L0_gnn_Wk_w, L0_gnn_Wk_b, L0_gnn_rule_emb, L0_gnn_bias, L0_gnn_ln_gamma, L0_gnn_ln_beta, L0_gnn_rule_ids):
    import jax
    import jax.numpy as jnp

    def _L0_gnn_ref(x, W_r, Wq_w, Wq_b, Wk_w, Wk_b, rule_emb, bias, ln_gamma, ln_beta, src, dst, edge_type, rule_ids):
        import jax, jax.numpy as jnp
        import numpy as np
        N = 3750
        E = 120000
        DIN = 128
        DOUT = 128
        R = 32
        NUM_RULES = 100
        ACTIVE = 4
        EPS = 1e-05
        n_nodes, _ = x.shape
        n_rel, _, dout = W_r.shape
        scale = 1.0 / jnp.sqrt(jnp.float32(dout))
        h_R = rule_emb[rule_ids]
        q = (x @ Wq_w + Wq_b)[dst]
        Wk1, Wk2, Wk3 = jnp.split(Wk_w, 3, axis=0)
        h_rel = W_r.mean(axis=-1)
        k_node = x @ Wk1
        k_rel = h_rel @ Wk2
        v_rule = h_R @ Wk3
        k_base = k_node[src] + k_rel[edge_type] + Wk_b
        score_base = jnp.sum(q * k_base, axis=-1)
        scores = (score_base[:, None] + q @ v_rule.T) * scale
        seg = edge_type * n_nodes + dst
        nseg = n_rel * n_nodes
        m = jax.ops.segment_max(scores, seg, num_segments=nseg)
        ex = jnp.exp(scores - m[seg])
        s = jax.ops.segment_sum(ex, seg, num_segments=nseg)
        attn = ex / s[seg]
        attn_mean = attn.mean(axis=-1)
        proj = jnp.einsum('nd,rdo->nro', x, W_r)
        msg = proj[src, edge_type] * attn_mean[:, None]
        out = jax.ops.segment_sum(msg, dst, num_segments=n_nodes) + bias
        mu = out.mean(axis=-1, keepdims=True)
        var = out.var(axis=-1, keepdims=True)
        out = (out - mu) * jax.lax.rsqrt(var + EPS) * ln_gamma + ln_beta
        return jax.nn.relu(out)
    h = jnp.maximum(_layernorm(x, axis=-1), 0.0)
    x = x + _L0_gnn_ref(h, L0_gnn_W_r, L0_gnn_Wq_w, L0_gnn_Wq_b, L0_gnn_Wk_w, L0_gnn_Wk_b, L0_gnn_rule_emb, L0_gnn_bias, L0_gnn_ln_gamma, L0_gnn_ln_beta, src, dst, edge_type_32, L0_gnn_rule_ids)
    return x

_drawn_inputs = setup_inputs


def setup_inputs(seed=0):
    import zlib

    import numpy as np

    out = dict(_drawn_inputs(seed))
    spreads = {'L0_gnn_Wq_b': (0.0, 0.8),
     'L0_gnn_Wk_b': (0.0, 0.8),
     'L0_gnn_bias': (0.0, 0.1),
     'L0_gnn_ln_gamma': (1.0, 0.2),
     'L0_gnn_ln_beta': (0.0, 0.1)}
    factors = {'L0_gnn_Wq_w': 3.642, 'L0_gnn_Wk_w': 3.512, 'L0_gnn_rule_emb': 8.0}
    for name, (base, spread) in spreads.items():
        noise = np.random.default_rng([zlib.crc32(name.encode()), seed]).standard_normal(out[name].shape)
        drawn = base * np.exp(spread * noise) if base else spread * noise
        out[name] = jnp.asarray(drawn.astype(out[name].dtype))
    for name, factor in factors.items():
        out[name] = (out[name] * factor).astype(out[name].dtype)
    return out
```

```python
from contextlib import ExitStack

import concourse.bass as bass
from concourse import mybir

P = 128
D = 128
N = 12500
E = 212500
R = 32
A = 4
NB = -(-N // P)
NP = NB * P
TG = 2
GE = TG * P
U = 8
NG = -(-(-(-E // GE) + NB) // U) * U
LEAD = 12
NGP = max(NG + LEAD, P)
QW = D + R + A
SAMPLE = 512
NSAMP = -(-E // SAMPLE)
LB = 7
BIG = 1.0e38
EPS = 1e-5
PAD_DST = NB * P + 456
SCALE = 1.0 / (128.0 ** 0.5)


class Group:

    def __init__(self, i, n):
        self.g = i * U + n if not isinstance(i, int) else i * U + n
        self.slot, self.round = n % U, i + (n // U + 1)
        self.pair, self.pround = n % 2, i * (U // 2) + (n // 2 + 1)


def pipeline(eng, steps):
    for base in range(-max(lag for _, lag in steps), 0):
        for stage, lag in steps:
            if base + lag >= 0:
                stage(Group(0, base + lag))
    with eng.Fori(0, NG // U) as i:
        for j in range(U):
            for stage, lag in steps:
                stage(Group(i, j + lag))


def build(nc, x, meta, samples, dst_rows, w_r, wq, wq_b, wk, wk_b, rule_emb, rule_ids,
          bias, gamma, beta, out):
    f32, i32 = mybir.dt.float32, mybir.dt.int32
    ALU, ACT, AX = mybir.AluOpType, mybir.ActivationFunctionType, mybir.AxisListType

    h_tab = nc.dram_tensor("h_tab", (NP, D), f32, kind="Internal").ap()
    q_tab = nc.dram_tensor("q_tab", ((NB + 1) * P, QW), f32, kind="Internal").ap()
    proj_tab = nc.dram_tensor("proj_tab", (NP, R * D), f32, kind="Internal").ap()
    proj_rows = proj_tab.rearrange("n (r o) -> (n r) o", r=R)
    ms_tab = nc.dram_tensor("ms_tab", ((NB + 1) * P, 2 * A * R), f32, kind="Internal").ap()
    lse_tab = nc.dram_tensor("lse_tab", ((NB + 1) * P, A * R), f32, kind="Internal").ap()
    prime_tab = nc.dram_tensor("prime_tab", (16, 8), f32, kind="Internal").ap()
    agg_tab = nc.dram_tensor("agg_tab", ((NB + 1) * P, D), f32, kind="Internal").ap()

    with ExitStack() as ctx:
        def sb(name, shape, dt=f32):
            return ctx.enter_context(nc.sbuf_tensor(name, shape, dt))

        def sem(name):
            return ctx.enter_context(nc.semaphore(name))

        ident = sb("ident", [P, P])
        ones = sb("ones", [P, P])
        zeros = sb("zeros", [P, 2 * A * R])
        iota_n = sb("iota_n", [P, P])
        iota_g = sb("iota_g", [P, NGP])
        first_node = sb("first_node", [P, 1])
        first_node_i = sb("first_node_i", [P, 1], i32)
        eps = sb("eps", [P, 1])
        w_sb = sb("w_sb", [P, R * D])
        wq_sb = sb("wq_sb", [P, D])
        wk_sb = sb("wk_sb", [P, 3, D])
        wqb_sb = sb("wqb_sb", [P, 1])
        wkb_sb = sb("wkb_sb", [P, 1])
        ids_sb = sb("ids_sb", [A, 1], i32)
        rules_sb = sb("rules_sb", [A, D])
        rulesT_sb = sb("rulesT_sb", [P, A])
        hrelT_sb = sb("hrelT_sb", [P, R])
        qw_sb = sb("qw_sb", [P, QW])
        bias_sb = sb("bias_sb", [P, D])
        gamma_sb = sb("gamma_sb", [P, D])
        beta_sb = sb("beta_sb", [P, D])
        coarse = sb("coarse", [P, 1])
        chunk = sb("chunk", [P, 1])
        chunk_i = sb("chunk_i", [P, 1], i32)
        fine = sb("fine", [P, 1])
        start_col = sb("start_col", [P, 1])
        start_row = sb("start_row", [P, P])
        cnt_i = sb("cnt_i", [P, NB], i32)
        groups_i = sb("groups_i", [P, NB], i32)
        groups = sb("groups", [P, P])
        gend = sb("gend", [P, P])
        kshift = sb("kshift", [P, P])
        kstep = sb("kstep", [P, P])
        gend_col = sb("gend_col", [P, 1])
        kstep_col = sb("kstep_col", [P, 1])
        blk = sb("blk", [P, NGP])
        blk128 = sb("blk128", [P, NGP])
        keep = sb("keep", [P, NGP])
        e0_i = sb("e0_i", [1, NGP], i32)
        blk_i = sb("blk_i", [1, NGP], i32)
        dlocs = sb("dlocs", [P, NGP * TG])
        ets = sb("ets", [P, NGP * TG])
        idx2s = sb("idx2s", [P, NGP * TG], i32)
        scores = sb("scores", [P, NGP * TG, A])
        xt = sb("xt", [P, 2, D])
        stats = sb("stats", [P, 2, 6])
        mv = sb("mv", [P, 2, 2])
        std = sb("std", [P, 2, 1])
        rstd = sb("rstd", [P, 2, 1])
        ostats = sb("ostats", [P, 2, LB, 6])
        omv = sb("omv", [P, 2, LB, 2])
        ostd = sb("ostd", [P, 2, LB])
        orstd = sb("orstd", [P, 2, LB])
        hc = sb("hc", [P, 2, D])
        h = sb("h", [P, 2, D])
        hT = sb("hT", [P, 2, P])
        qT = sb("qT", [P, 2, P])
        qt = sb("qt", [P, 2, QW])
        proj = sb("proj", [P, 2, R * D])
        scratch = [0]

        def carve(width, dt=f32):
            at = scratch[0]
            scratch[0] += width
            return proj[:, :, :].rearrange("p a b -> p (a b)")[:, at:at + width].bitcast(dt)

        iota_gi = carve(NGP, i32)
        passed = carve(NGP)
        e0f = carve(NGP)[0:1, :]
        samp_sb = carve(NSAMP, i32)
        fine_sb = carve(SAMPLE, i32)
        below = carve(SAMPLE)
        samp_f = carve(SAMPLE)
        meta_sb = sb("meta_sb", [P, U, TG, 5], i32)
        rows = sb("rows", [P, U, TG, D + R])
        onehot = sb("onehot", [P, U, TG, P])
        caprel = sb("caprel", [P, U, TG, R])
        capnew = sb("capnew", [P, U, TG])
        last = sb("last", [P, U, TG])
        qblk = sb("qblk", [P, 2, QW])
        ohT = sb("ohT", [P, 2, TG * P])
        dots = sb("dots", [P, 2, TG])
        prod = sb("prod", [P, 2, TG, D + R])
        masked = sb("masked", [P, 2, TG, A * R])
        capT = sb("capT", [P, 2, GE])
        fmax = sb("fmax", [P, 2, GE + 1])
        before = sb("before", [P, GE])
        diff = sb("diff", [P, 2, 2 * GE])
        expd = sb("expd", [P, 2, 2 * GE])
        ssum = sb("ssum", [P, 2, GE + 1])
        ms_last = sb("ms_last", [P, 2, TG, 2 * A * R])
        ms_acc = sb("ms_acc", [P, 2, 2 * A * R])
        lblk = sb("lblk", [P, 2, A * R])
        idx2 = sb("idx2", [P, U, TG], i32)
        picked = sb("picked", [P, 2, TG, A, R])
        lse = sb("lse", [P, 2, TG, A])
        z = sb("z", [P, 2, TG, A])
        ez = sb("ez", [P, 2, TG, A])
        wsum = sb("wsum", [P, 2, TG])
        msg = sb("msg", [P, 2, TG, D])
        agg_acc = sb("agg_acc", [P, 2, D])

        bank = [ctx.enter_context(nc.psum_tensor(f"bank{k}", [P, 512], f32)) for k in range(8)]

        c_ident = sem("c_ident")
        c_zeros = sem("c_zeros")
        w_in = [sem(f"w_in{k}") for k in range(10)]
        chunk_ready = sem("chunk_ready")
        fine_in = sem("fine_in")
        rules_in = sem("rules_in")
        zero_out = sem("zero_out")
        vchain = sem("vchain")
        achain = sem("achain")
        start_ready = sem("start_ready")
        startT = sem("startT")
        gend_ready = sem("gend_ready")
        gendT = sem("gendT")
        passed_ready = sem("passed_ready")
        blkp = sem("blkp")
        sched_ready = sem("sched_ready")
        rulesTp = sem("rulesTp")
        rulesT = sem("rulesT")
        qwp = sem("qwp")
        qw_ready = sem("qw_ready")
        sp_go = sem("sp_go")
        x_in = [sem(f"x_in{k}") for k in range(2)]
        n_stats = sem("n_stats")
        n_seen = sem("n_seen")
        n_mv = sem("n_mv")
        n_std = sem("n_std")
        n_rstd = sem("n_rstd")
        n_hc = sem("n_hc")
        n_h = sem("n_h")
        n_hTp = sem("n_hTp")
        n_hT = sem("n_hT")
        n_qTp = sem("n_qTp")
        n_qT = sem("n_qT")
        n_qtp = sem("n_qtp")
        n_qt = sem("n_qt")
        n_pp = [sem(f"n_pp{k}") for k in range(4)]
        n_pc = [sem(f"n_pc{k}") for k in range(4)]
        h_out = [sem(f"h_out{k}") for k in range(2)]
        qt_out = [sem(f"qt_out{k}") for k in range(2)]
        proj_out = [sem(f"proj_out{k}") for k in range(2)]
        meta_in = [sem(f"meta_in{k}") for k in range(U)]
        rows_in = [sem(f"rows_in{k}") for k in range(U)]
        qblk_in = [sem(f"qblk_in{k}") for k in range(2)]
        pool_go = sem("pool_go")
        s_dloc = sem("s_dloc")
        s_ohr = sem("s_ohr")
        s_isnew = sem("s_isnew")
        s_prep = sem("s_prep")
        s_ohTp = sem("s_ohTp")
        s_ohT = sem("s_ohT")
        s_qexp = sem("s_qexp")
        s_dot = sem("s_dot")
        s_x4 = sem("s_x4")
        s_mask = sem("s_mask")
        s_maskT = sem("s_maskT")
        s_capTp = sem("s_capTp")
        s_capT = sem("s_capT")
        s_max = sem("s_max")
        s_maxcarry = sem("s_maxcarry")
        s_before = sem("s_before")
        s_diff = sem("s_diff")
        s_exp = sem("s_exp")
        s_sum = sem("s_sum")
        s_sumcarry = sem("s_sumcarry")
        s_msTp = sem("s_msTp")
        s_msT = sem("s_msT")
        s_msp = sem("s_msp")
        s_ms = sem("s_ms")
        ms_out = sem("ms_out")
        l_in = [sem(f"l_in{k}") for k in range(2)]
        l_out = [sem(f"l_out{k}") for k in range(2)]
        l_pos = sem("l_pos")
        l_ln = sem("l_ln")
        l_sum = sem("l_sum")
        m_idx = sem("m_idx")
        m_rows_in = [sem(f"m_rows_in{k}") for k in range(U)]
        lblk_in = [sem(f"lblk_in{k}") for k in range(2)]
        m_oh = sem("m_oh")
        m_ohTp = sem("m_ohTp")
        m_ohT = sem("m_ohT")
        m_lexp = sem("m_lexp")
        m_pick = sem("m_pick")
        m_lse = sem("m_lse")
        m_z = sem("m_z")
        m_w = sem("m_w")
        m_msg = sem("m_msg")
        m_aggp = sem("m_aggp")
        m_agg = sem("m_agg")
        agg_out = sem("agg_out")
        o_in = [sem(f"o_in{k}") for k in range(2)]
        o_out = [sem(f"o_out{k}") for k in range(2)]
        o_mv = sem("o_mv")
        o_std = sem("o_std")
        o_done = sem("o_done")

        block = ctx.enter_context(nc.Block())

        @block.sync
        def _(sp):
            loads = [
                (w_sb[:, :].rearrange("d (r o) -> d r o", r=R), w_r.rearrange("r d o -> d r o")),
                (wq_sb[:, :], wq),
                (wk_sb[:, :, :], wk.rearrange("(s d) o -> d s o", s=3)),
                (wqb_sb[:, :], wq_b.rearrange("(o a) -> o a", a=1)),
                (wkb_sb[:, :], wk_b.rearrange("(o a) -> o a", a=1)),
                (ids_sb[:, :], rule_ids.rearrange("(o a) -> o a", a=1)),
                (bias_sb[:, :], bias.rearrange("(a o) -> a o", a=1).to_broadcast([P, D])),
                (gamma_sb[:, :], gamma.rearrange("(a o) -> a o", a=1).to_broadcast([P, D])),
                (beta_sb[:, :], beta.rearrange("(a o) -> a o", a=1).to_broadcast([P, D])),
                (samp_sb[:, :], samples.rearrange("(a o) -> a o", a=1).to_broadcast([P, NSAMP])),
            ]
            for k, (to, source) in reversed(list(enumerate(loads))):
                sp.dma_start(to, source).then_inc(w_in[k], 16)

            sp.wait_ge(c_zeros, 1)
            primed = [agg_out, *h_out, *qt_out, *proj_out, *l_out, *o_out, agg_out]
            for k, s in enumerate(primed):
                if k == len(primed) - 1:
                    sp.wait_ge(agg_out, 16)
                sp.dma_start(prime_tab[k:k + 1, :], zeros[0:1, 0:8]).then_inc(s, 16)
            sp.dma_start(q_tab[NB * P:NB * P + 64, :], zeros[0:64, 0:QW]).then_inc(ms_out, 16)
            sp.wait_ge(ms_out, 16)
            sp.dma_start(q_tab[NB * P + 64:(NB + 1) * P, :], zeros[0:64, 0:QW]).then_inc(ms_out, 16)
            sp.dma_start(lse_tab[NB * P:(NB + 1) * P, :], zeros[:, 0:A * R]).then_inc(zero_out, 16)
            for b in range(0, NB, LB):
                part = slice(b * P, (b + LB) * P)
                sp.dma_start(ms_tab[part, :].rearrange("(b p) c -> p b c", p=P),
                             zeros[:, None, :].to_broadcast([P, LB, 2 * A * R])).then_inc(zero_out, 16)
                sp.dma_start(agg_tab[part, :].rearrange("(b p) c -> p b c", p=P),
                             zeros[:, None, 0:D].to_broadcast([P, LB, D])).then_inc(zero_out, 16)

            def load_x(t, j):
                sp.wait_ge(n_hc, t + 1)
                sp.dma_start(xt[:, j, :], x[bass.ds(t * P, P), :]).then_inc(x_in[j], 16)

            def store_tables(t, j):
                sp.wait_ge(n_h, t + 1)
                sp.dma_start(h_tab[bass.ds(t * P, P), :], h[:, j, :]).then_inc(h_out[j], 16)
                sp.wait_ge(n_qt, t + 1)
                sp.dma_start(q_tab[bass.ds(t * P, P), :], qt[:, j, :]).then_inc(qt_out[j], 16)
                for c in range(4):
                    sp.wait_ge(n_pc[c], 2 * t + 3)
                sp.dma_start(proj_tab[bass.ds(t * P, P), :], proj[:, j, :]).then_inc(proj_out[j], 16)

            load_x(0, 0)
            load_x(1, 1)
            with sp.Fori(0, NB // 2) as i:
                for j in range(2):
                    load_x(i * 2 + (j + 2), j)
                    store_tables(i * 2 + j, j)

            for k in range(2):
                sp.wait_ge(qt_out[k], 16 * (NB // 2 + 1))
            sp.wait_ge(zero_out, 16 * (2 * (NB // LB) + 1))
            sp.wait_ge(ms_out, 32)
            sp.wait_ge(sched_ready, 1)

            def load_edges(G):
                e0 = sp.value_load(e0_i[0:1, bass.ds(G.g, 1)], min_val=0, max_val=E)
                sp.wait_ge(s_dot, G.g + 1)
                sp.wait_ge(s_prep, G.g + 1)
                sp.dma_start(meta_sb[:, G.slot, :, :],
                             meta[bass.ds(e0, GE), :].rearrange("(t p) c -> p t c", t=TG)
                             ).then_inc(meta_in[G.slot], 16)

            def load_q(G):
                b = sp.value_load(blk_i[0:1, bass.ds(G.g, 1)], min_val=0, max_val=NB)
                sp.wait_ge(s_qexp, G.g + 1)
                sp.dma_start(qblk[:, G.pair, :], q_tab[bass.ds(b * P, P), :]).then_inc(qblk_in[G.pair], 16)

            def store_ms(G):
                b = sp.value_load(blk_i[0:1, bass.ds(G.g, 1)], min_val=0, max_val=NB)
                sp.wait_ge(ms_out, (G.g + 2) * 16)
                sp.wait_ge(s_ms, G.g + 2)
                sp.dma_start(ms_tab[bass.ds(b * P, P), :], ms_acc[:, G.pair, :]).then_inc(ms_out, 16)

            pipeline(sp, [(load_edges, 10), (load_q, 6), (store_ms, 0)])
            sp.wait_ge(ms_out, (NG + 2) * 16)
            for k in range(U):
                sp.wait_ge(meta_in[k], 16 * len(range(k, NG + 10, U)))
            for k in range(2):
                sp.wait_ge(qblk_in[k], 16 * len(range(k, NG + 6, 2)))

            def lse_rows(tab, t):
                return tab[bass.ds(t * (LB * P), LB * P), :].rearrange("(b p) c -> p b c", p=P)

            with sp.Fori(0, NB // LB // 2) as i:
                for j in range(2):
                    t = i * 2 + j
                    sp.wait_ge(l_sum, t + 1)
                    sp.dma_start(proj[:, j, 0:LB * 2 * A * R].rearrange("p (b c) -> p b c", b=LB),
                                 lse_rows(ms_tab, t)).then_inc(l_in[j], 16)
                    sp.wait_ge(l_sum, t + 3)
                    sp.dma_start(lse_rows(lse_tab, t),
                                 proj[:, j, 3072:3072 + LB * A * R].rearrange("p (b c) -> p b c", b=LB)
                                 ).then_inc(l_out[j], 16)
            for k in range(2):
                sp.wait_ge(l_out[k], 16 * (NB // LB // 2 + 1))

            def load_lse(G):
                b = sp.value_load(blk_i[0:1, bass.ds(G.g, 1)], min_val=0, max_val=NB)
                sp.wait_ge(m_lexp, G.g + 1)
                sp.dma_start(lblk[:, G.pair, :], lse_tab[bass.ds(b * P, P), :]).then_inc(lblk_in[G.pair], 16)

            def store_agg(G):
                b = sp.value_load(blk_i[0:1, bass.ds(G.g, 1)], min_val=0, max_val=NB)
                sp.wait_ge(agg_out, (G.g + 2) * 16)
                sp.sem_inc(sp_go, 1)
                sp.wait_ge(m_agg, G.g + 3)
                sp.dma_start(agg_tab[bass.ds(b * P, P), :], agg_acc[:, G.pair, :]).then_inc(agg_out, 16)

            pipeline(sp, [(load_lse, 5), (store_agg, 0)])
            sp.wait_ge(agg_out, (NG + 2) * 16)
            for k in range(2):
                sp.wait_ge(lblk_in[k], 16 * len(range(k, NG + 5, 2)))

            with sp.Fori(0, NB // LB // 2) as i:
                for j in range(2):
                    t = i * 2 + j
                    sp.wait_ge(o_done, t + 1)
                    for half, tab in ((0, agg_tab), (1, x)):
                        sp.dma_start(proj[:, j, half * 1024:half * 1024 + LB * D]
                                     .rearrange("p (b c) -> p b c", b=LB),
                                     lse_rows(tab, t)).then_inc(o_in[j], 16)
                    sp.wait_ge(o_done, t + 3)
                    sp.dma_start(lse_rows(out, t), proj[:, j, 3072:3072 + LB * D]
                                 .rearrange("p (b c) -> p b c", b=LB)).then_inc(o_out[j], 16)
            for k in range(2):
                sp.wait_ge(o_out[k], 16 * (NB // LB // 2 + 1))

        @block.gpsimd
        def _(pool):
            nc.gpsimd.memset(zeros[:, :], 0.0).then_inc(c_zeros, 1)
            nc.gpsimd.memset(ident[:, :], 0.0).then_inc(c_ident, 1)
            pool.wait_ge(c_ident, 1)
            nc.gpsimd.affine_select(out=ident[:, :], in_=ident[:, :], compare_op=ALU.not_equal,
                                    fill=1.0, base=0, pattern=[[-1, P]],
                                    channel_multiplier=1).then_inc(c_ident, 1)
            nc.gpsimd.iota(first_node_i[:, :], pattern=[[0, 1]], base=0,
                           channel_multiplier=P).then_inc(c_ident, 1)
            nc.gpsimd.iota(iota_gi[:, :], pattern=[[1, NGP]], base=0,
                           channel_multiplier=0).then_inc(c_ident, 1)
            pool.wait_ge(w_in[5], 16)
            pool.indirect_dma_start(rules_sb[:, :], None, rule_emb,
                                    bass.IndirectOffsetOnAxis(ids_sb[:, 0:1], 0)).then_inc(rules_in, 16)
            pool.wait_ge(chunk_ready, 1)
            pool.indirect_dma_start(fine_sb[:, :], None, dst_rows,
                                    bass.IndirectOffsetOnAxis(chunk_i[:, 0:1], 0)).then_inc(fine_in, 16)

            for k in range(2):
                pool.wait_ge(h_out[k], 16 * (NB // 2 + 1))

            def gather_h(G):
                pool.wait_ge(meta_in[G.slot], G.round * 16)
                pool.sem_inc(pool_go, 1)
                pool.wait_ge(s_dot, G.g + 1)
                pool.sem_inc(pool_go, 1)
                for t in range(TG):
                    pool.indirect_dma_start(rows[:, G.slot, t, 0:D], None, h_tab,
                                            bass.IndirectOffsetOnAxis(meta_sb[:, G.slot, t, 0:1], 0)
                                            ).then_inc(rows_in[G.slot], 16)
            pipeline(pool, [(gather_h, 4)])

            for k in range(2):
                pool.wait_ge(proj_out[k], 16 * (NB // 2 + 1))

            def gather_proj(G):
                pool.wait_ge(m_idx, G.g + 1)
                pool.sem_inc(pool_go, 1)
                pool.wait_ge(m_msg, G.g + 1)
                pool.sem_inc(pool_go, 1)
                for t in range(TG):
                    pool.indirect_dma_start(rows[:, G.slot, t, 0:D], None, proj_rows,
                                            bass.IndirectOffsetOnAxis(idx2[:, G.slot, t:t + 1], 0)
                                            ).then_inc(m_rows_in[G.slot], 16)
            pipeline(pool, [(gather_proj, 2)])

        @block.scalar
        def _(act):
            act.sem_inc(s_ohT, 1)
            act.sem_inc(s_capT, 1)
            act.sem_inc(s_exp, 2)
            act.sem_inc(s_msT, U)
            act.sem_inc(m_ohT, 1)
            act.sem_inc(m_w, 2)
            act.sem_inc(m_msg, U)
            act.sem_inc(n_pc[0], 1)
            act.sem_inc(n_pc[2], 1)
            act.wait_ge(vchain, 2)
            for k in (3,):
                act.wait_ge(w_in[k], 16)

            def deviation(t, j):
                act.wait_ge(n_mv, t + 1)
                nc.scalar.activation(std[:, j, :], mv[:, j, 1:2], ACT.Sqrt, bias=eps[:, :]
                                     ).then_inc(n_std, 1)

            def copy_hT(t, j):
                act.wait_ge(n_hTp, t + 1)
                nc.scalar.activation(hT[:, j, :], bank[0][:, 0:P], ACT.Copy).then_inc(n_hT, 1)

            def node_copies(t, j):
                for c in (0, 2, 4, 6):
                    if c == 4:
                        act.wait_ge(n_qTp, t + 1)
                        nc.scalar.activation(qT[:, j, :], bank[1][:, 0:P], ACT.Identity,
                                             bias=wqb_sb[:, :]).then_inc(n_qT, 1)
                    if c == 6:
                        copy_hT(t + 1, 1 - j)
                    if c == 0:
                        act.wait_ge(proj_out[j], proj_round(t, j))
                    act.wait_ge(n_pp[c % 4], 2 * t + (c // 4 + 1))
                    nc.scalar.activation(proj[:, j, c * 512:(c + 1) * 512], bank[4 + c % 4][:, :],
                                         ACT.Copy).then_inc(n_pc[c % 4], 1)

            def proj_round(t, j):
                return node_round[0] * 16

            node_round = [0]
            deviation(0, 0)
            copy_hT(0, 0)
            with act.Fori(0, NB // 2) as i:
                node_round[0] = i + 1
                for j in range(2):
                    deviation(i * 2 + (j + 1), (j + 1) % 2)
                    node_copies(i * 2 + j, j)

            def copy_ohT(G):
                act.wait_ge(s_ohTp, G.g + 1)
                act.wait_ge(s_qexp, G.g + 1)
                nc.scalar.activation(ohT[:, G.pair, :], bank[0][:, 0:GE], ACT.Copy).then_inc(s_ohT, 1)

            def copy_capT(G):
                act.wait_ge(s_capTp, G.g + 1 + U)
                act.wait_ge(s_before, G.g + 1)
                nc.scalar.activation(capT[:, G.pair, :], bank[5][:, 0:GE], ACT.Copy).then_inc(s_capT, 1)

            def exponentials(G):
                act.wait_ge(s_diff, G.g + 3)
                act.wait_ge(s_sum, G.g + 1)
                nc.scalar.activation(expd[:, G.pair, :], diff[:, G.pair, :], ACT.Exp).then_inc(s_exp, 1)

            def keep_last(G):
                act.wait_ge(s_msTp, G.g + 3)
                act.wait_ge(s_msp, G.g + U - 1)
                for t in range(TG):
                    done = nc.scalar.activation(ms_last[:, G.pair, t, :],
                                                bank[6][:, t * 256:(t + 1) * 256], ACT.Copy,
                                                scale=last[:, G.slot, t:t + 1])
                done.then_inc(s_msT, 1)

            pipeline(act, [(exponentials, 2), (copy_ohT, 5), (keep_last, 1), (copy_capT, 3)])

            with act.Fori(0, NB // LB // 2) as i:
                for j in range(2):
                    t = i * 2 + j
                    act.wait_ge(l_pos, t + 1)
                    nc.scalar.activation(proj[:, j, 2048:2048 + LB * A * R],
                                         proj[:, j, 2048:2048 + LB * A * R], ACT.Ln).then_inc(l_ln, 1)

            def copy_idx(G):
                nc.scalar.activation(idx2[:, G.slot, :], idx2s[:, bass.ds(G.g * TG, TG)],
                                     ACT.Copy).then_inc(m_idx, 1)

            def copy_moh(G):
                act.wait_ge(m_ohTp, G.g + 1)
                act.wait_ge(m_lexp, G.g + 1)
                nc.scalar.activation(ohT[:, G.pair, :], bank[0][:, 0:GE], ACT.Copy).then_inc(m_ohT, 1)

            def weights(G):
                act.wait_ge(m_z, G.g + 1)
                for t in range(TG):
                    done = nc.scalar.activation(ez[:, G.pair, t, :], z[:, G.pair, t, :], ACT.Exp,
                                                accum_out=wsum[:, G.pair, t:t + 1])
                done.then_inc(m_w, 1)

            def messages(G):
                act.wait_ge(m_rows_in[G.slot], G.round * 32)
                act.wait_ge(m_aggp, G.g + U - 1)
                act.wait_ge(m_w, G.g + 3)
                for t in range(TG):
                    done = nc.scalar.activation(msg[:, G.pair, t, :], rows[:, G.slot, t, 0:D],
                                                ACT.Copy, scale=wsum[:, G.pair, t:t + 1])
                done.then_inc(m_msg, 1)

            pipeline(act, [(copy_moh, 4), (weights, 2), (messages, 2), (copy_idx, 8)])

            with act.Fori(0, NB // LB // 2) as i:
                for j in range(2):
                    t = i * 2 + j
                    act.wait_ge(o_mv, t + 1)
                    nc.scalar.activation(ostd[:, j, :], omv[:, j, :, 1], ACT.Sqrt, bias=eps[:, :]
                                         ).then_inc(o_std, 1)

        @block.tensor
        def _(pe):
            pe.sem_inc(s_qexp, 2)
            pe.sem_inc(s_capTp, U)
            pe.sem_inc(s_msTp, 2)
            pe.sem_inc(s_msp, U)
            pe.sem_inc(m_lexp, 2)
            pe.sem_inc(m_aggp, U)
            pe.wait_ge(c_ident, 4)
            pe.wait_ge(rules_in, 16)
            nc.tensor.transpose(bank[6][:, 0:A], rules_sb[:, :], ident[0:A, 0:A]).then_inc(rulesTp, 1)
            pe.wait_ge(start_ready, 1)
            nc.tensor.matmul(bank[0][:, 0:P], start_col[:, 0:1].to_broadcast([P, P]), ident[:, :],
                             start=True, stop=True).then_inc(startT, 1)
            pe.wait_ge(gend_ready, 2)
            nc.tensor.transpose(bank[1][0:NB, 0:P], gend[:, 0:NB], ident[:, :])
            nc.tensor.transpose(bank[1][0:NB, P:2 * P], kstep[:, 0:NB], ident[:, :]).then_inc(gendT, 1)
            pe.wait_ge(passed_ready, 1)
            for c in range(2):
                part = slice(c * NGP // 2, (c + 1) * NGP // 2)
                nc.tensor.matmul(bank[2 + c][:, 0:NGP // 2], ones[0:NB, :], passed[0:NB, part],
                                 start=True, stop=True)
                done = nc.tensor.matmul(bank[4 + c][0:1, 0:NGP // 2], kstep_col[0:NB, :],
                                        passed[0:NB, part], start=True, stop=True)
            done.then_inc(blkp, 1)
            pe.wait_ge(w_in[2], 16)
            nc.tensor.transpose(bank[7][:, 0:D], wk_sb[:, 0, :], ident[:, :])
            pe.wait_ge(rulesT, 2)
            nc.tensor.matmul(bank[7][:, D:D + R], wk_sb[:, 1, :], hrelT_sb[:, :], start=True, stop=True)
            nc.tensor.matmul(bank[7][:, D + R:QW], wk_sb[:, 2, :], rulesT_sb[:, :], start=True,
                             stop=True).then_inc(qwp, 1)
            pe.wait_ge(qw_ready, 1)
            pe.wait_ge(sched_ready, 1)
            pe.wait_ge(w_in[0], 16)
            pe.wait_ge(w_in[1], 16)

            def transpose_h(t, j):
                pe.wait_ge(n_h, t + 1)
                nc.tensor.transpose(bank[0][:, 0:P], h[:, j, :], ident[:, :]).then_inc(n_hTp, 1)

            def node_products(t, j):
                pe.wait_ge(n_hT, t + 1)
                for c in range(R * D // 512):
                    if c == 3:
                        nc.tensor.matmul(bank[1][:, 0:P], wq_sb[:, :], hT[:, j, :], start=True,
                                         stop=True).then_inc(n_qTp, 1)
                    if c == 5:
                        transpose_h(t + 1, 1 - j)
                    if c == 7:
                        pe.wait_ge(n_qT, t + 1)
                        nc.tensor.matmul(bank[2][:, 0:QW], qT[:, j, :], qw_sb[:, :], start=True,
                                         stop=True).then_inc(n_qtp, 1)
                    pe.wait_ge(n_pc[c % 4], 2 * t + (c // 4 + 1))
                    nc.tensor.matmul(bank[4 + c % 4][:, :], hT[:, j, :],
                                     w_sb[:, c * 512:(c + 1) * 512], start=True,
                                     stop=True).then_inc(n_pp[c % 4], 1)

            transpose_h(0, 0)
            with pe.Fori(0, NB // 2) as i:
                for j in range(2):
                    node_products(i * 2 + j, j)
            for c in range(4):
                pe.wait_ge(n_pc[c], 2 * NB + 1)
            pe.wait_ge(n_qt, NB)

            def transpose_onehot(G):
                pe.wait_ge(s_prep, G.g + 1 + U)
                pe.wait_ge(s_ohT, G.g + 1)
                for t in range(TG):
                    done = nc.tensor.transpose(bank[0][:, t * P:(t + 1) * P], onehot[:, G.slot, t, :],
                                               ident[:, :])
                done.then_inc(s_ohTp, 1)

            def expand_q(G):
                pe.wait_ge(s_ohT, G.g + 2)
                pe.wait_ge(qblk_in[G.pair], G.pround * 16)
                pe.wait_ge(s_x4, G.g + 1)
                for t in range(TG):
                    done = nc.tensor.matmul(bank[1 + G.pair][:, t * 256:t * 256 + QW],
                                            ohT[:, G.pair, t * P:(t + 1) * P], qblk[:, G.pair, :],
                                            start=True, stop=True)
                done.then_inc(s_qexp, 1)

            def transpose_masked(G):
                pe.wait_ge(s_mask, G.g + 1 + U)
                pe.wait_ge(s_diff, G.g + 2)
                for t in range(TG):
                    done = nc.tensor.transpose(bank[3][:, t * P:(t + 1) * P], masked[:, G.pair, t, :],
                                               ident[:, :])
                done.then_inc(s_maskT, 1)
                pe.wait_ge(s_capT, G.g + 1)
                for t in range(TG):
                    done = nc.tensor.transpose(bank[5][:, t * P:(t + 1) * P],
                                               capnew[:, G.slot, t:t + 1].to_broadcast([P, P]),
                                               ident[:, :])
                done.then_inc(s_capTp, 1)

            def transpose_ms(G):
                pe.wait_ge(s_sum, G.g + 3)
                pe.wait_ge(s_msT, G.g + U)
                for t in range(TG):
                    for q, source in enumerate((fmax, ssum)):
                        done = nc.tensor.transpose(
                            bank[6][:, t * 256 + q * P:t * 256 + (q + 1) * P],
                            source[:, G.pair, 1 + t * P:1 + (t + 1) * P], ident[:, :])
                done.then_inc(s_msTp, 1)

            def place_ms(G):
                pe.wait_ge(s_msT, G.g + 1 + U)
                pe.wait_ge(s_ms, G.g + 1)
                for t in range(TG):
                    done = nc.tensor.matmul(bank[7][:, 0:2 * A * R], onehot[:, G.slot, t, :],
                                            ms_last[:, G.pair, t, :], start=(t == 0), stop=(t == TG - 1))
                done.then_inc(s_msp, 1)

            pipeline(pe, [(transpose_onehot, 5), (transpose_ms, 1), (transpose_masked, 3),
                          (place_ms, 0), (expand_q, 5)])

            def transpose_moh(G):
                pe.wait_ge(m_oh, G.g + 1)
                pe.wait_ge(m_ohT, G.g + 1)
                for t in range(TG):
                    done = nc.tensor.transpose(bank[0][:, t * P:(t + 1) * P], onehot[:, G.slot, t, :],
                                               ident[:, :])
                done.then_inc(m_ohTp, 1)

            def expand_lse(G):
                pe.wait_ge(m_ohT, G.g + 2)
                pe.wait_ge(lblk_in[G.pair], G.pround * 16)
                pe.wait_ge(m_pick, G.g + U - 1)
                for t in range(TG):
                    done = nc.tensor.matmul(bank[1 + G.pair][:, t * P:(t + 1) * P],
                                            ohT[:, G.pair, t * P:(t + 1) * P], lblk[:, G.pair, :],
                                            start=True, stop=True)
                done.then_inc(m_lexp, 1)

            def aggregate(G):
                pe.wait_ge(m_msg, G.g + 1 + U)
                pe.wait_ge(m_agg, G.g + 1)
                for t in range(TG):
                    done = nc.tensor.matmul(bank[3 + G.pair][:, 0:D], onehot[:, G.slot, t, :],
                                            msg[:, G.pair, t, :], start=(t == 0), stop=(t == TG - 1))
                done.then_inc(m_aggp, 1)

            pipeline(pe, [(transpose_moh, 4), (aggregate, 1), (expand_lse, 4)])

        @block.vector
        def _(dve):
            steps = [0]

            def chain(ins):
                steps[0] += 1
                ins.then_inc(vchain, 1)
                dve.wait_ge(vchain, steps[0])

            V = nc.vector
            chain(V.memset(ones[:, :], 1.0))
            chain(V.memset(eps[:, :], EPS))
            dve.sem_inc(n_pc[1], 1)
            dve.sem_inc(n_pc[3], 1)
            dve.sem_inc(n_hc, 2)
            dve.sem_inc(s_prep, U)
            dve.sem_inc(s_dot, U)
            dve.sem_inc(s_x4, 2)
            dve.sem_inc(s_mask, U)
            dve.sem_inc(s_before, 2)
            dve.sem_inc(s_diff, 1 + 1)
            dve.sem_inc(s_sum, 2)
            dve.sem_inc(s_ms, 1)
            dve.sem_inc(l_sum, 2)
            dve.sem_inc(m_pick, U)
            dve.sem_inc(m_agg, 2)
            dve.sem_inc(o_done, 2)
            dve.wait_ge(c_ident, 4)
            chain(V.tensor_copy(first_node[:, :], first_node_i[:, :]))
            chain(V.tensor_copy(iota_g[:, :], iota_gi[:, :]))

            dve.wait_ge(w_in[9], 16)
            chain(V.tensor_copy(samp_f[:, 0:NSAMP], samp_sb[:, :]))
            chain(V.tensor_scalar(below[:, 0:NSAMP], samp_f[:, 0:NSAMP], first_node[:, :], None,
                                  ALU.is_lt, ALU.add, accum_out=coarse[:, :]))
            chain(V.tensor_scalar(chunk[:, :], coarse[:, :], -1.0, 0.0, ALU.add, ALU.max))
            V.tensor_copy(chunk_i[:, :], chunk[:, :]).then_inc(chunk_ready, 1)
            dve.wait_ge(fine_in, 16)
            chain(V.tensor_copy(samp_f[:, :], fine_sb[:, :]))
            chain(V.tensor_scalar(below[:, :], samp_f[:, :], first_node[:, :], None,
                                  ALU.is_lt, ALU.add, accum_out=fine[:, :]))
            V.scalar_tensor_tensor(out=start_col[:, :], in0=chunk[:, :], scalar=float(SAMPLE),
                                   in1=fine[:, :], op0=ALU.mult, op1=ALU.add).then_inc(start_ready, 1)
            dve.wait_ge(startT, 1)
            chain(V.tensor_copy(start_row[:, :], bank[0][:, 0:P]))
            chain(V.scalar_tensor_tensor(out=cnt_i[:, :], in0=start_row[:, 1:NB + 1],
                                         scalar=float(GE - 1), in1=start_row[:, 0:NB],
                                         op0=ALU.add, op1=ALU.subtract))
            chain(V.tensor_scalar(groups_i[:, :], cnt_i[:, :], GE.bit_length() - 1, None,
                                  ALU.arith_shift_right))
            chain(V.tensor_copy(groups[:, 0:NB], groups_i[:, :]))
            V.tensor_tensor_scan(gend[:, 0:NB], ones[:, 0:NB], groups[:, 0:NB], 0.0, ALU.mult,
                                 ALU.add).then_inc(gend_ready, 1)
            dve.wait_ge(gend_ready, 1)
            chain(V.tensor_tensor(out=groups[:, 0:NB], in0=gend[:, 0:NB], in1=groups[:, 0:NB],
                                  op=ALU.subtract))
            chain(V.scalar_tensor_tensor(out=kshift[:, 0:NB], in0=groups[:, 0:NB],
                                         scalar=-float(GE), in1=start_row[:, 0:NB], op0=ALU.mult,
                                         op1=ALU.add))
            chain(V.scalar_tensor_tensor(out=kshift[:, NB:NB + 1], in0=gend[:, NB - 1:NB],
                                         scalar=-float(GE), in1=start_row[:, NB:NB + 1],
                                         op0=ALU.mult, op1=ALU.add))
            V.tensor_tensor(out=kstep[:, 0:NB], in0=kshift[:, 1:NB + 1], in1=kshift[:, 0:NB],
                            op=ALU.subtract).then_inc(gend_ready, 1)
            dve.wait_ge(gendT, 1)
            chain(V.tensor_copy(gend_col[0:NB, :], bank[1][0:NB, 0:1]))
            chain(V.tensor_copy(kstep_col[0:NB, :], bank[1][0:NB, P:P + 1]))
            V.tensor_scalar(passed[0:NB, :], iota_g[0:NB, :], gend_col[0:NB, :], None,
                            ALU.is_ge).then_inc(passed_ready, 1)
            dve.wait_ge(blkp, 1)
            for c in range(2):
                part = slice(c * NGP // 2, (c + 1) * NGP // 2)
                chain(V.tensor_copy(blk[:, part], bank[2 + c][:, 0:NGP // 2]))
                chain(V.scalar_tensor_tensor(out=e0f[:, part], in0=iota_g[0:1, part],
                                             scalar=float(GE), in1=bank[4 + c][0:1, 0:NGP // 2],
                                             op0=ALU.mult, op1=ALU.add))
            chain(V.tensor_scalar(e0_i[:, :], e0f[:, :], float(E), None, ALU.min))
            chain(V.tensor_copy(blk_i[:, :], blk[0:1, :]))
            chain(V.tensor_scalar(blk128[:, :], blk[:, :], float(P), None, ALU.mult))
            chain(V.memset(keep[:, 0:1], 0.0))
            V.tensor_tensor(out=keep[:, 1:NGP], in0=blk[:, 1:NGP], in1=blk[:, 0:NGP - 1],
                            op=ALU.is_equal).then_inc(sched_ready, 1)

            dve.wait_ge(rulesTp, 1)
            V.tensor_copy(rulesT_sb[:, :], bank[6][:, 0:A]).then_inc(rulesT, 1)
            dve.wait_ge(w_in[0], 16)
            chain(V.tensor_reduce(hrelT_sb[:, :], w_sb[:, :].rearrange("d (r o) -> d r o", r=R),
                                  AX.X, ALU.add))
            V.tensor_scalar(hrelT_sb[:, :], hrelT_sb[:, :], 1.0 / D, None, ALU.mult).then_inc(rulesT, 1)
            dve.wait_ge(qwp, 1)
            dve.wait_ge(w_in[4], 16)
            chain(V.tensor_copy(qw_sb[:, :], bank[7][:, 0:QW]))
            V.tensor_scalar(qw_sb[:, D:D + R], qw_sb[:, D:D + R], wkb_sb[:, :], None,
                            ALU.add).then_inc(qw_ready, 1)
            chain(V.memset(idx2s[:, NG * TG:], 0))
            chain(V.memset(fmax[:, 0, 0:1], -BIG))
            chain(V.memset(ssum[:, 0, 0:1], 0.0))
            chain(V.memset(ms_acc[:, :, :], 0.0))
            chain(V.memset(agg_acc[:, :, :], 0.0))

            def normalize(t, j, rnd):
                dve.wait_ge(x_in[j], rnd * 16)
                V.bn_stats(stats[:, j, :], xt[:, j, :]).then_inc(n_stats, 1)
                dve.wait_ge(n_stats, t + 1)
                dve.sem_inc(n_seen, 1)
                V.bn_aggr(mv[:, j, :], stats[:, j, :]).then_inc(n_mv, 1)
                dve.wait_ge(n_std, t + 1)
                V.reciprocal(rstd[:, j, :], std[:, j, :]).then_inc(n_rstd, 1)
                dve.wait_ge(n_rstd, t + 1)
                V.tensor_scalar(hc[:, j, :], xt[:, j, :], mv[:, j, 0:1], rstd[:, j, :],
                                ALU.subtract, ALU.mult).then_inc(n_hc, 1)
                dve.wait_ge(n_hc, t + 3)
                dve.wait_ge(h_out[j], rnd * 16)
                V.tensor_scalar(h[:, j, :], hc[:, j, :], 0.0, None, ALU.max).then_inc(n_h, 1)

            def node_evacuate(t, j, rnd):
                for c in (1, 3, 5, 7):
                    if c == 7:
                        dve.wait_ge(n_qtp, t + 1)
                        dve.wait_ge(qt_out[j], rnd * 16)
                        V.tensor_copy(qt[:, j, :], bank[2][:, 0:QW]).then_inc(n_qt, 1)
                    if c == 1:
                        dve.wait_ge(proj_out[j], rnd * 16)
                    dve.wait_ge(n_pp[c % 4], 2 * t + (c // 4 + 1))
                    V.tensor_copy(proj[:, j, c * 512:(c + 1) * 512], bank[4 + c % 4][:, :]
                                  ).then_inc(n_pc[c % 4], 1)

            normalize(0, 0, 1)
            with dve.Fori(0, NB // 2) as i:
                normalize(i * 2 + 1, 1, i + 1)
                node_evacuate(i * 2, 0, i + 1)
                normalize(i * 2 + 2, 0, i + 2)
                node_evacuate(i * 2 + 1, 1, i + 1)

            def edge_masks(G):
                edge = meta_sb[:, G.slot, :, :]
                dloc = dlocs[:, bass.ds(G.g * TG, TG)]
                et = ets[:, bass.ds(G.g * TG, TG)]
                dve.wait_ge(meta_in[G.slot], G.round * 16)
                V.tensor_tensor(out=dloc, in0=edge[:, :, 3],
                                in1=blk128[:, bass.ds(G.g, 1)].to_broadcast([P, TG]),
                                op=ALU.subtract).then_inc(s_dloc, 1)
                V.tensor_copy(et, edge[:, :, 1]).then_inc(s_dloc, 1)
                V.scalar_tensor_tensor(out=idx2s[:, bass.ds(G.g * TG, TG)], in0=edge[:, :, 0],
                                       scalar=float(R), in1=edge[:, :, 1], op0=ALU.mult, op1=ALU.add)
                dve.wait_ge(s_capTp, G.g + 1)
                V.tensor_tensor(out=capnew[:, G.slot, :], in0=edge[:, :, 3], in1=edge[:, :, 2],
                                op=ALU.is_equal).then_inc(s_isnew, 1)
                dve.wait_ge(s_dot, G.g + 1)
                V.tensor_tensor(out=rows[:, G.slot, :, D:D + R],
                                in0=iota_g[:, None, 0:R].to_broadcast([P, TG, R]),
                                in1=edge[:, :, 1:2].to_broadcast([P, TG, R]),
                                op=ALU.is_equal).then_inc(s_ohr, 1)
                dve.wait_ge(s_msT, G.g + 1)
                V.tensor_tensor(out=last[:, G.slot, :], in0=edge[:, :, 3], in1=edge[:, :, 4],
                                op=ALU.not_equal)
                dve.wait_ge(s_isnew, G.g + 1)
                V.tensor_scalar(capnew[:, G.slot, :], capnew[:, G.slot, :], 2 * BIG, -BIG,
                                ALU.mult, ALU.add)
                dve.wait_ge(s_dloc, G.g * 2 + 2)
                dve.wait_ge(s_msp, G.g + 1)
                V.tensor_tensor(out=onehot[:, G.slot, :, :],
                                in0=iota_g[:, None, 0:P].to_broadcast([P, TG, P]),
                                in1=dloc[:, :, None].to_broadcast([P, TG, P]), op=ALU.is_equal)
                dve.wait_ge(s_ohr, G.g + 1)
                dve.wait_ge(s_mask, G.g + 1)
                V.tensor_scalar(caprel[:, G.slot, :, :], rows[:, G.slot, :, D:D + R], 2 * BIG, -BIG,
                                ALU.mult, ALU.add).then_inc(s_prep, 1)

            def score(G):
                q = bank[1 + G.pair]
                dve.wait_ge(rows_in[G.slot], G.round * 32)
                dve.wait_ge(s_qexp, G.g + 3)
                for t in range(TG):
                    done = V.tensor_tensor_reduce(
                        out=prod[:, G.pair, t, :], in0=q[:, t * 256:t * 256 + D + R],
                        in1=rows[:, G.slot, t, :], scale=1.0, scalar=0.0, op0=ALU.mult, op1=ALU.add,
                        accum_out=dots[:, G.pair, t:t + 1])
                done.then_inc(s_dot, 1)
                dve.wait_ge(s_dot, G.g + 1 + U)
                for t in range(TG):
                    done = V.tensor_scalar(scores[:, bass.ds(G.g * TG + t, 1), :],
                                           q[:, t * 256 + D + R:t * 256 + QW],
                                           dots[:, G.pair, t:t + 1], SCALE, ALU.add, ALU.mult)
                done.then_inc(s_x4, 1)
                dve.wait_ge(s_x4, G.g + 3)
                dve.wait_ge(s_prep, G.g + 1 + U)
                V.tensor_tensor(
                    out=masked[:, G.pair, :, :].rearrange("p t (a r) -> p t a r", a=A),
                    in0=scores[:, bass.ds(G.g * TG, TG), :, None].to_broadcast([P, TG, A, R]),
                    in1=caprel[:, G.slot, :, None, :].to_broadcast([P, TG, A, R]),
                    op=ALU.min).then_inc(s_mask, 1)

            def running_max(G):
                f, cap, lanes = fmax[:, G.pair, :], capT[:, G.pair, :], bank[3][:, 0:GE]
                dve.wait_ge(s_maskT, G.g + 1)
                dve.wait_ge(s_capT, G.g + 2)
                dve.wait_ge(s_msTp, G.g + 1)
                if not (isinstance(G.g, int) and G.g == 0):
                    dve.wait_ge(s_maxcarry, G.g)
                V.tensor_tensor_scan(f[:, 1:GE + 1], cap, lanes, f[:, 0:1], ALU.min,
                                     ALU.max).then_inc(s_max, 1)
                dve.wait_ge(s_max, G.g + 1)
                dve.wait_ge(s_exp, G.g + 1)
                V.tensor_copy(fmax[:, 1 - G.pair, 0:1], f[:, GE:GE + 1]).then_inc(s_maxcarry, 1)
                V.tensor_tensor(out=before[:, :], in0=f[:, 0:GE], in1=cap, op=ALU.min
                                ).then_inc(s_before, 1)
                V.tensor_tensor(out=diff[:, G.pair, GE:2 * GE], in0=lanes, in1=f[:, 1:GE + 1],
                                op=ALU.subtract)
                dve.wait_ge(s_before, G.g + 3)
                V.tensor_tensor(out=diff[:, G.pair, 0:GE], in0=before[:, :], in1=f[:, 1:GE + 1],
                                op=ALU.subtract).then_inc(s_diff, 1)

            def running_sum(G):
                s = ssum[:, G.pair, :]
                dve.wait_ge(s_exp, G.g + 3)
                dve.wait_ge(s_msTp, G.g + 1)
                if not (isinstance(G.g, int) and G.g == 0):
                    dve.wait_ge(s_sumcarry, G.g + 1)
                V.tensor_tensor_scan(s[:, 1:GE + 1], expd[:, G.pair, 0:GE], expd[:, G.pair, GE:2 * GE],
                                     s[:, 0:1], ALU.mult, ALU.add).then_inc(s_sum, 1)
                dve.wait_ge(s_sum, G.g + 3)
                V.tensor_copy(ssum[:, 1 - G.pair, 0:1], s[:, GE:GE + 1]).then_inc(s_sumcarry, 1)

            def accumulate_ms(G):
                dve.wait_ge(s_msp, G.g + 1 + U)
                dve.wait_ge(ms_out, (G.g + 1) * 16)
                dve.wait_ge(s_ms, G.g + 1)
                V.scalar_tensor_tensor(out=ms_acc[:, G.pair, :], in0=ms_acc[:, 1 - G.pair, :],
                                       scalar=keep[:, bass.ds(G.g, 1)], in1=bank[7][:, 0:2 * A * R],
                                       op0=ALU.mult, op1=ALU.add).then_inc(s_ms, 1)

            dve.sem_inc(s_sumcarry, 1)
            pipeline(dve, [(running_max, 2), (edge_masks, 6), (score, 4), (running_sum, 2),
                           (accumulate_ms, 0)])

            with dve.Fori(0, NB // LB // 2) as i:
                for j in range(2):
                    t = i * 2 + j
                    ms = proj[:, j, 0:LB * 2 * A * R].rearrange("p (b c) -> p b c", b=LB)
                    tmp = proj[:, j, 2048:2048 + LB * A * R].rearrange("p (b c) -> p b c", b=LB)
                    dve.wait_ge(l_in[j], (i + 1) * 16)
                    V.tensor_scalar(tmp, ms[:, :, A * R:], 1e-30, None, ALU.max).then_inc(l_pos, 1)
                    dve.wait_ge(l_ln, t + 1)
                    dve.wait_ge(l_out[j], (i + 1) * 16)
                    V.tensor_tensor(out=proj[:, j, 3072:3072 + LB * A * R]
                                    .rearrange("p (b c) -> p b c", b=LB),
                                    in0=ms[:, :, 0:A * R], in1=tmp, op=ALU.add).then_inc(l_sum, 1)

            def message_masks(G):
                dve.wait_ge(m_pick, G.g + 1)
                V.tensor_tensor(out=rows[:, G.slot, :, D:D + R],
                                in0=iota_g[:, None, 0:R].to_broadcast([P, TG, R]),
                                in1=ets[:, bass.ds(G.g * TG, TG), None].to_broadcast([P, TG, R]),
                                op=ALU.is_equal)
                dve.wait_ge(m_aggp, G.g + 1)
                V.tensor_tensor(out=onehot[:, G.slot, :, :],
                                in0=iota_g[:, None, 0:P].to_broadcast([P, TG, P]),
                                in1=dlocs[:, bass.ds(G.g * TG, TG), None].to_broadcast([P, TG, P]),
                                op=ALU.is_equal).then_inc(m_oh, 1)

            def exponents(G):
                dve.wait_ge(m_lexp, G.g + 3)
                dve.wait_ge(m_oh, G.g + 1)
                dve.wait_ge(m_lse, G.g + 1)
                V.tensor_tensor(out=picked[:, G.pair, :, :, :],
                                in0=bank[1 + G.pair][:, 0:GE].rearrange("p (t a r) -> p t a r", t=TG, a=A),
                                in1=rows[:, G.slot, :, None, D:D + R].to_broadcast([P, TG, A, R]),
                                op=ALU.mult).then_inc(m_pick, 1)
                dve.wait_ge(m_pick, G.g + 1 + U)
                V.tensor_reduce(lse[:, G.pair, :, :], picked[:, G.pair, :, :, :], AX.X, ALU.add
                                ).then_inc(m_lse, 1)
                dve.wait_ge(m_lse, G.g + 2)
                dve.wait_ge(m_w, G.g + 1)
                V.tensor_tensor(out=z[:, G.pair, :, :], in0=scores[:, bass.ds(G.g * TG, TG), :],
                                in1=lse[:, G.pair, :, :], op=ALU.subtract).then_inc(m_z, 1)

            def accumulate_agg(G):
                dve.wait_ge(m_aggp, G.g + 1 + U)
                dve.wait_ge(agg_out, (G.g + 1) * 16)
                dve.wait_ge(m_agg, G.g + 2)
                V.scalar_tensor_tensor(out=agg_acc[:, G.pair, :], in0=agg_acc[:, 1 - G.pair, :],
                                       scalar=keep[:, bass.ds(G.g, 1)], in1=bank[3 + G.pair][:, 0:D],
                                       op0=ALU.mult, op1=ALU.add).then_inc(m_agg, 1)

            dve.sem_inc(m_lse, 1)
            pipeline(dve, [(exponents, 3), (message_masks, 5), (accumulate_agg, 0)])

            base = steps[0]
            OSTEPS = 7
            with dve.Fori(0, NB // LB // 2) as i:
                for j in range(2):
                    t = i * 2 + j
                    n = [0]

                    def ochain(ins):
                        n[0] += 1
                        ins.then_inc(vchain, 1)
                        dve.wait_ge(vchain, t * OSTEPS + (base + n[0]))

                    def wide(v):
                        return v.rearrange("p (b c) -> p b c", b=LB)
                    agg = wide(proj[:, j, 0:LB * D])
                    res = wide(proj[:, j, 1024:1024 + LB * D])
                    y = wide(proj[:, j, 2048:2048 + LB * D])
                    o = wide(proj[:, j, 3072:3072 + LB * D])
                    full = [P, LB, D]
                    dve.wait_ge(o_in[j], (i + 1) * 32)
                    ochain(V.scalar_tensor_tensor(out=y, in0=agg, scalar=1.0 / A,
                                                  in1=bias_sb[:, None, :].to_broadcast(full),
                                                  op0=ALU.mult, op1=ALU.add))
                    for b in range(LB):
                        done = V.bn_stats(ostats[:, j, b, :], y[:, b, :])
                    ochain(done)
                    dve.sem_inc(n_seen, 1)
                    for b in range(LB):
                        done = V.bn_aggr(omv[:, j, b, :], ostats[:, j, b, :])
                    done.then_inc(o_mv, 1)
                    dve.wait_ge(o_mv, t + 1)
                    dve.wait_ge(o_std, t + 1)
                    V.reciprocal(orstd[:, j, :], ostd[:, j, :])
                    ochain(V.tensor_tensor(out=y, in0=y, in1=omv[:, j, :, 0:1].to_broadcast(full),
                                           op=ALU.subtract))
                    ochain(V.tensor_tensor(out=y, in0=y, in1=orstd[:, j, :, None].to_broadcast(full),
                                           op=ALU.mult))
                    ochain(V.tensor_tensor(out=y, in0=y, in1=gamma_sb[:, None, :].to_broadcast(full),
                                           op=ALU.mult))
                    ochain(V.tensor_tensor(out=y, in0=y, in1=beta_sb[:, None, :].to_broadcast(full),
                                           op=ALU.add))
                    dve.wait_ge(o_out[j], (i + 1) * 16)
                    ochain(V.scalar_tensor_tensor(out=o, in0=y, scalar=0.0, in1=res, op0=ALU.max,
                                                  op1=ALU.add))
                    dve.sem_inc(o_done, 1)


def kernel(**inputs):
    import numpy as np
    import concourse.bacc as bacc
    from concourse.bass_utils import run_bass_kernel_spmd

    x = np.ascontiguousarray(inputs["x"])
    xpad = np.zeros(((NB + 2) * P, D), x.dtype)
    xpad[:N] = x
    src, dst, et = (np.ascontiguousarray(inputs[k]) for k in ("src", "dst", "edge_type_32"))
    meta = np.zeros((E + GE, 5), src.dtype)
    meta[:, 2:5] = PAD_DST
    meta[:E, 0] = src
    meta[:E, 1] = et
    meta[:E, 3] = dst
    meta[0, 2] = -1
    meta[1:E + 1, 2] = dst
    meta[:E - 1, 4] = dst[1:]
    rows = np.full((NSAMP, SAMPLE), PAD_DST, dst.dtype)
    rows.reshape(-1)[:E] = dst
    arrays = {"x": xpad, "meta": meta, "samples": np.ascontiguousarray(rows[:, 0]), "dst_rows": rows}
    for name in ("W_r", "Wq_w", "Wq_b", "Wk_w", "Wk_b", "rule_emb", "rule_ids", "bias", "ln_gamma",
                 "ln_beta"):
        arrays[name] = np.ascontiguousarray(inputs["L0_gnn_" + name])

    nc = bacc.Bacc("TRN2", target_bir_lowering=False, num_devices=1)
    args = [nc.dram_tensor("in_" + n, a.shape, mybir.dt.from_np(a.dtype), kind="ExternalInput").ap()
            for n, a in arrays.items()]
    out = nc.dram_tensor("out_0", (NP, D), mybir.dt.float32, kind="ExternalOutput").ap()
    build(nc, *args, out)
    r = run_bass_kernel_spmd(nc, [{"in_" + n: a for n, a in arrays.items()}], core_ids=[0])
    return r.results[0]["out_0"][:N]
```

```python
from contextlib import ExitStack

import concourse.bass as bass
from concourse import mybir

P = 128
D = 128
N = 12500
E = 212500
R = 32
A = 4
NB = -(-N // P)
NP = NB * P
TG = 2
GE = TG * P
U = 8
T = 3 * U
NG = -(-(-(-E // GE) + NB) // T) * T
LEAD = 12
NGP = max(NG + LEAD, P)
QW = D + R + A
SAMPLE = 512
NSAMP = -(-E // SAMPLE)
NBX = -(-NB // (T // U)) * (T // U)
NODES = 14
LB = 7
BIG = 2.0 ** 126
EPS = 1e-5
PAD_DST = NB * P + 456
SCALE = 1.0 / (128.0 ** 0.5)


class Group:

    def __init__(self, i, n):
        self.g = i * T + n
        self.slot, self.round = n % U, i * (T // U) + (n // U + 1)
        self.pair, self.pround = n % 2, i * (T // 2) + (n // 2 + 1)
        self.quad, self.next_quad, self.qround = n % 4, (n + 1) % 4, i * (T // 4) + (n // 4 + 1)


def pipeline(eng, steps, beside=None, beside_at=0):
    for base in range(-max(lag for _, lag in steps), 0):
        for stage, lag in steps:
            if base + lag >= 0:
                stage(Group(0, base + lag))
    both = NBX // (T // U)
    for first, end, extra in ((0, both, True), (both, NG // T, False)) if beside else ((0, NG // T, False),):
        with eng.Fori(first, end) as i:
            for j in range(T):
                for k, (stage, lag) in enumerate(steps):
                    if extra and k == beside_at:
                        beside(i * (T // U) + j // U, j % U)
                    stage(Group(i, j + lag))


def build(nc, x, meta, samples, dst_rows, w_r, wq, wq_b, wk, wk_b, rule_emb, rule_ids,
          bias, gamma, beta, out):
    f32, i32 = mybir.dt.float32, mybir.dt.int32
    ALU, ACT, AX = mybir.AluOpType, mybir.ActivationFunctionType, mybir.AxisListType

    h_tab = nc.dram_tensor("h_tab", (NP + P, D), f32, kind="Internal").ap()
    q_tab = nc.dram_tensor("q_tab", ((NB + 1) * P, QW), f32, kind="Internal").ap()
    proj_tab = nc.dram_tensor("proj_tab", (NBX * P, R * D), f32, kind="Internal").ap()
    proj_rows = proj_tab.rearrange("n (r o) -> (n r) o", r=R)
    ms_tab = nc.dram_tensor("ms_tab", ((NB + 1) * P, 2 * A * R), f32, kind="Internal").ap()
    lse_tab = nc.dram_tensor("lse_tab", ((NB + 1) * P, A * R), f32, kind="Internal").ap()
    prime_tab = nc.dram_tensor("prime_tab", (16, 8), f32, kind="Internal").ap()
    agg_tab = nc.dram_tensor("agg_tab", ((NB + 5) * P, D), f32, kind="Internal").ap()

    with ExitStack() as ctx:
        def sb(name, shape, dt=f32):
            return ctx.enter_context(nc.sbuf_tensor(name, shape, dt))

        def sem(name):
            return ctx.enter_context(nc.semaphore(name))

        ident = sb("ident", [P, P])
        ones = sb("ones", [P, P])
        zeros = sb("zeros", [P, 2 * A * R])
        iota = sb("iota", [P, P])
        first_node = sb("first_node", [P, 1])
        first_node_i = sb("first_node_i", [P, 1], i32)
        eps = sb("eps", [P, 1])
        w_sb = sb("w_sb", [P, R * D])
        wq_sb = sb("wq_sb", [P, D])
        wqb_sb = sb("wqb_sb", [P, 1])
        wkb_sb = sb("wkb_sb", [P, 1])
        ids_sb = sb("ids_sb", [A, 1], i32)
        rules_sb = sb("rules_sb", [A, D])
        rulesT_sb = sb("rulesT_sb", [P, A])
        hrelT_sb = sb("hrelT_sb", [P, R])
        qw_sb = sb("qw_sb", [P, QW])
        bias_sb = sb("bias_sb", [P, D])
        gamma_sb = sb("gamma_sb", [P, D])
        beta_sb = sb("beta_sb", [P, D])
        coarse = sb("coarse", [P, 1])
        chunk = sb("chunk", [P, 1])
        chunk_i = sb("chunk_i", [P, 1], i32)
        fine = sb("fine", [P, 1])
        start_col = sb("start_col", [P, 1])
        gend_col = sb("gend_col", [P, 1])
        kstep_col = sb("kstep_col", [P, 1])
        blk128 = sb("blk128", [P, NGP])
        keep = sb("keep", [P, NGP])
        e0_i = sb("e0_i", [1, NGP], i32)
        blk_i = sb("blk_i", [1, NGP], i32)
        store_i = sb("store_i", [1, NGP], i32)
        dlocs = sb("dlocs", [P, NGP * TG])
        ets = sb("ets", [P, NGP * TG], mybir.dt.bfloat16)
        idx2s = sb("idx2s", [P, NGP * TG], i32)
        scores = sb("scores", [P, NGP * TG, A])
        stats = sb("stats", [P, 2, 6])
        mv = sb("mv", [P, 2, 2])
        std = sb("std", [P, 2, 1])
        rstd = sb("rstd", [P, 2, 1])
        ostats = sb("ostats", [P, 2, LB, 6])
        omv = sb("omv", [P, 2, LB, 2])
        ostd = sb("ostd", [P, 2, LB])
        orstd = sb("orstd", [P, 2, LB])
        hTs = sb("hTs", [P, max((NBX + 1) * P, 2 * 4096 + 2048)])
        hT = sb("hT", [P, P])
        proj = sb("proj", [P, 2, R * D // 2])
        wide_sb = hTs[:, 0:2 * 4096].rearrange("p (j c) -> p j c", j=2)
        scratch = [0]

        def carve(width, dt=f32):
            at = scratch[0]
            scratch[0] += width
            return hTs[:, at:at + width].bitcast(dt)

        iota_gi = carve(NGP, i32)
        iota_g = carve(NGP)
        blk = carve(NGP)
        passed = carve(NGP)
        e0f = carve(NGP)[0:1, :]
        samp_sb = carve(NSAMP, i32)
        fine_sb = carve(SAMPLE, i32)
        below = carve(SAMPLE)
        samp_f = carve(SAMPLE)
        start_row, groups, gend, kshift, kstep = (carve(P) for _ in range(5))
        cnt_i, groups_i = carve(NB, i32), carve(NB, i32)
        meta_sb = sb("meta_sb", [P, U, TG, 5], i32)
        rows = sb("rows", [P, U, TG, D + R])
        onehot = sb("onehot", [P, U, TG, P])
        caprel = sb("caprel", [P, U, TG, R])
        ends = sb("ends", [P, U, TG, 2])
        capnew = sb("capnew", [P, U, TG], mybir.dt.bfloat16)
        ident_b = sb("ident_b", [P, P], mybir.dt.bfloat16)
        qblk = sb("qblk", [P, 2, QW])
        ohT = sb("ohT", [P, 2, TG * P])
        dots = sb("dots", [P, 2, TG])
        prod = sb("prod", [P, 2, TG, D + R])
        masked = sb("masked", [P, 2, TG, A * R])
        capT = sb("capT", [P, 2, GE])
        fmax = sb("fmax", [P, 4, GE + 1])
        diff = sb("diff", [P, 2, 2 * GE])
        expd = sb("expd", [P, 2, 2 * GE])
        ssum = sb("ssum", [P, 2, GE + 1])
        ms_last = sb("ms_last", [P, 2, TG, 2 * A * R])
        ms_acc = sb("ms_acc", [P, 2, 2 * A * R])
        idx2 = sb("idx2", [P, U, TG], i32)
        lse = sb("lse", [P, 2, TG, A])
        z = sb("z", [P, 2, TG, A])
        ez = sb("ez", [P, 2, TG, A])
        wsum = sb("wsum", [P, 2, TG])

        late = hTs[:, 2 * 4096:2 * 4096 + 2048]
        lblk = late[:, 0:512].rearrange("p (s c) -> p s c", s=4)
        picked = late[:, 512:1024].rearrange("p (s t a r) -> p s t a r", s=2, t=TG, a=A)
        msg = late[:, 1024:1536].rearrange("p (s t c) -> p s t c", s=2, t=TG)
        agg_acc = late[:, 1536:2048].rearrange("p (s c) -> p s c", s=4)
        early = diff[:, :, :].rearrange("p s c -> p (s c)")
        xt, hc, h, hT2 = (early[:, k * 256:(k + 1) * 256].rearrange("p (s c) -> p s c", s=2)
                          for k in range(4))
        early = expd[:, :, :].rearrange("p s c -> p (s c)")
        qT = early[:, 0:256].rearrange("p (s c) -> p s c", s=2)
        qt = early[:, 256:256 + 2 * QW].rearrange("p (s c) -> p s c", s=2)
        wk_sb = early[:, 640:640 + 3 * D].rearrange("p (s c) -> p s c", s=3)

        bank = [ctx.enter_context(nc.psum_tensor(f"bank{k}", [P, 512], f32)) for k in range(8)]

        c_ident = sem("c_ident")
        c_zeros = sem("c_zeros")
        w_in = [sem(f"w_in{k}") for k in range(10)]
        chunk_ready = sem("chunk_ready")
        fine_in = sem("fine_in")
        rules_in = sem("rules_in")
        zero_out = sem("zero_out")
        vchain = sem("vchain")
        start_ready = sem("start_ready")
        startT = sem("startT")
        gend_ready = sem("gend_ready")
        gendT = sem("gendT")
        passed_ready = sem("passed_ready")
        blkp = sem("blkp")
        sched_ready = sem("sched_ready")
        rulesTp = sem("rulesTp")
        rulesT = sem("rulesT")
        qwp = sem("qwp")
        qw_ready = sem("qw_ready")
        x_in = [sem(f"x_in{k}") for k in range(2)]
        n_stats = sem("n_stats")
        n_seen = sem("n_seen")
        n_mv = sem("n_mv")
        n_std = sem("n_std")
        n_rstd = sem("n_rstd")
        n_hc = sem("n_hc")
        n_h = sem("n_h")
        n_hTp = sem("n_hTp")
        n_hT = sem("n_hT")
        n_hT2 = sem("n_hT2")
        n_qTp = sem("n_qTp")
        n_qT = sem("n_qT")
        n_qtp = sem("n_qtp")
        n_qt = sem("n_qt")
        p_hT = sem("p_hT")
        p_prod = sem("p_prod")
        p_copied = sem("p_copied")
        h_out = [sem(f"h_out{k}") for k in range(2)]
        qt_out = [sem(f"qt_out{k}") for k in range(2)]
        proj_out = [sem(f"proj_out{k}") for k in range(2)]
        meta_in = [sem(f"meta_in{k}") for k in range(U)]
        rows_in = [sem(f"rows_in{k}") for k in range(U)]
        qblk_in = [sem(f"qblk_in{k}") for k in range(2)]
        pool_go = sem("pool_go")
        s_dloc = sem("s_dloc")
        s_et = sem("s_et")
        s_ohr = sem("s_ohr")
        s_isnew = sem("s_isnew")
        s_prep = sem("s_prep")
        s_ohTp = sem("s_ohTp")
        s_ohT = sem("s_ohT")
        s_qexp = sem("s_qexp")
        s_dot = sem("s_dot")
        s_x4 = sem("s_x4")
        s_mask = sem("s_mask")
        s_maskT = sem("s_maskT")
        s_capTp = sem("s_capTp")
        s_capT = sem("s_capT")
        s_max = sem("s_max")
        s_maxcarry = sem("s_maxcarry")
        s_drop = sem("s_drop")
        s_diff = sem("s_diff")
        s_exp = sem("s_exp")
        s_sum = sem("s_sum")
        s_sumcarry = sem("s_sumcarry")
        s_decay = sem("s_decay")
        s_msTp = sem("s_msTp")
        s_msTp2 = sem("s_msTp2")
        s_msT = sem("s_msT")
        s_msp = sem("s_msp")
        s_ms = sem("s_ms")
        ms_out = sem("ms_out")
        l_in = [sem(f"l_in{k}") for k in range(2)]
        l_out = [sem(f"l_out{k}") for k in range(2)]
        l_pos = sem("l_pos")
        l_ln = sem("l_ln")
        l_sum = sem("l_sum")
        m_idx = sem("m_idx")
        m_rows_in = [sem(f"m_rows_in{k}") for k in range(U)]
        lblk_in = [sem(f"lblk_in{k}") for k in range(4)]
        m_oh = sem("m_oh")
        m_ohTp = sem("m_ohTp")
        m_ohT = sem("m_ohT")
        m_lexp = sem("m_lexp")
        m_pick = sem("m_pick")
        m_lse = sem("m_lse")
        m_z = sem("m_z")
        m_w = sem("m_w")
        m_msg = sem("m_msg")
        m_aggp = sem("m_aggp")
        m_agg = sem("m_agg")
        agg_out = [sem(f"agg_out{k}") for k in range(4)]
        o_in = [sem(f"o_in{k}") for k in range(2)]
        o_out = [sem(f"o_out{k}") for k in range(2)]
        o_mv = sem("o_mv")
        o_std = sem("o_std")
        o_done = sem("o_done")

        block = ctx.enter_context(nc.Block())

        @block.sync
        def _(sp):
            loads = [
                (w_sb[:, :].rearrange("d (r o) -> d r o", r=R), w_r.rearrange("r d o -> d r o")),
                (wq_sb[:, :], wq),
                (wk_sb[:, :, :], wk.rearrange("(s d) o -> d s o", s=3)),
                (wqb_sb[:, :], wq_b.rearrange("(o a) -> o a", a=1)),
                (wkb_sb[:, :], wk_b.rearrange("(o a) -> o a", a=1)),
                (ids_sb[:, :], rule_ids.rearrange("(o a) -> o a", a=1)),
                (bias_sb[:, :], bias.rearrange("(a o) -> a o", a=1).to_broadcast([P, D])),
                (gamma_sb[:, :], gamma.rearrange("(a o) -> a o", a=1).to_broadcast([P, D])),
                (beta_sb[:, :], beta.rearrange("(a o) -> a o", a=1).to_broadcast([P, D])),
                (samp_sb[:, :], samples.rearrange("(a o) -> a o", a=1).to_broadcast([P, NSAMP])),
            ]
            for k, (to, source) in reversed(list(enumerate(loads))):
                sp.dma_start(to, source).then_inc(w_in[k], 16)

            sp.wait_ge(c_zeros, 1)
            primed = [*agg_out, *h_out, *qt_out, *proj_out, *l_out, *o_out]
            for k, s in enumerate(primed):
                sp.dma_start(prime_tab[k:k + 1, :], zeros[0:1, 0:8]).then_inc(s, 16)
            sp.dma_start(q_tab[NB * P:NB * P + 64, :], zeros[0:64, 0:QW]).then_inc(ms_out, 16)
            sp.wait_ge(ms_out, 16)
            sp.dma_start(q_tab[NB * P + 64:(NB + 1) * P, :], zeros[0:64, 0:QW]).then_inc(ms_out, 16)
            sp.dma_start(lse_tab[NB * P:(NB + 1) * P, :], zeros[:, 0:A * R]).then_inc(zero_out, 16)
            for b in range(0, NB, LB):
                part = slice(b * P, (b + LB) * P)
                sp.dma_start(ms_tab[part, :].rearrange("(b p) c -> p b c", p=P),
                             zeros[:, None, :].to_broadcast([P, LB, 2 * A * R])).then_inc(zero_out, 16)
                sp.dma_start(agg_tab[part, :].rearrange("(b p) c -> p b c", p=P),
                             zeros[:, None, 0:D].to_broadcast([P, LB, D])).then_inc(zero_out, 16)

            def load_x(t, j):
                sp.wait_ge(n_hc, t + 1)
                sp.dma_start(xt[:, j, :], x[bass.ds(t * P, P), :]).then_inc(x_in[j], 16)

            def store_h(t, j):
                sp.wait_ge(n_h, t + 1)
                sp.dma_start(h_tab[bass.ds(t * P, P), :], h[:, j, :]).then_inc(h_out[j], 16)

            def store_q(t, j):
                sp.wait_ge(n_qt, t + 1)
                sp.dma_start(q_tab[bass.ds(t * P, P), :], qt[:, j, :]).then_inc(qt_out[j], 16)

            load_x(0, 0)
            load_x(1, 1)
            load_x(2, 0)
            store_h(0, 0)
            with sp.Fori(0, NB // NODES) as i:
                for j in range(NODES):
                    load_x(i * NODES + (j + 3), (j + 1) % 2)
                    store_h(i * NODES + (j + 1), (j + 1) % 2)
                    store_q(i * NODES + j, j % 2)

            for k in range(2):
                sp.wait_ge(qt_out[k], 16 * (NB // 2 + 1))
            sp.wait_ge(zero_out, 16 * (2 * (NB // LB) + 1))
            sp.wait_ge(ms_out, 32)
            sp.wait_ge(sched_ready, 1)

            held = {}

            def scheduled(stage, table, G, top):
                if G.slot % 4 == 0:
                    _, held[stage] = nc.values_load_multi_w_load_instructions(
                        table[0:1, bass.ds(G.g, 4)], engines=[mybir.EngineType.SP], min_val=0,
                        max_val=top)
                return held[stage][G.slot % 4]

            def load_edges(G):
                e0 = scheduled("edges", e0_i, G, E)
                sp.wait_ge(s_dot, G.g + 1)
                sp.wait_ge(s_prep, G.g + 1)
                sp.dma_start(meta_sb[:, G.slot, :, :],
                             meta[bass.ds(e0, GE), :].rearrange("(t p) c -> p t c", t=TG)
                             ).then_inc(meta_in[G.slot], 16)

            def load_q(G):
                b = scheduled("q", blk_i, G, NB)
                sp.wait_ge(s_qexp, G.g + 1)
                sp.dma_start(qblk[:, G.pair, :], q_tab[bass.ds(b * P, P), :]).then_inc(qblk_in[G.pair], 16)

            def store_ms(G):
                b = scheduled("ms", blk_i, G, NB)
                sp.wait_ge(ms_out, (G.g + 2) * 16)
                sp.wait_ge(s_ms, G.g + 2)
                sp.dma_start(ms_tab[bass.ds(b * P, P), :], ms_acc[:, G.pair, :]).then_inc(ms_out, 16)

            pipeline(sp, [(load_edges, 12), (load_q, 8), (store_ms, 0)])
            sp.wait_ge(ms_out, (NG + 2) * 16)
            for k in range(U):
                sp.wait_ge(meta_in[k], 16 * len(range(k, NG + 12, U)))
            for k in range(2):
                sp.wait_ge(qblk_in[k], 16 * len(range(k, NG + 8, 2)))

            sp.wait_ge(p_hT, NBX + 1)

            def block_rows(tab, t):
                return tab[bass.ds(t * (LB * P), LB * P), :].rearrange("(b p) c -> p b c", p=P)

            def one_ahead(load, store):
                count = NB // LB
                load(0, 0)
                if count > 2:
                    with sp.Fori(0, count // 2 - 1) as i:
                        for j in range(2):
                            load(i * 2 + (j + 1), 1 - j)
                            store(i * 2 + j, j)
                load(count - 1, 1)
                store(count - 2, 0)
                store(count - 1, 1)

            def load_ms(t, j):
                sp.wait_ge(l_sum, t + 1)
                sp.dma_start(wide_sb[:, j, 0:LB * 2 * A * R].rearrange("p (b c) -> p b c", b=LB),
                             block_rows(ms_tab, t)).then_inc(l_in[j], 16)

            def store_lse(t, j):
                sp.wait_ge(l_sum, t + 3)
                sp.dma_start(block_rows(lse_tab, t),
                             wide_sb[:, j, 3072:3072 + LB * A * R].rearrange("p (b c) -> p b c", b=LB)
                             ).then_inc(l_out[j], 16)

            one_ahead(load_ms, store_lse)
            for k in range(2):
                sp.wait_ge(l_out[k], 16 * (NB // LB // 2 + 1))

            def load_lse(G):
                b = scheduled("lse", blk_i, G, NB)
                sp.wait_ge(m_lexp, G.g + 1)
                sp.dma_start(lblk[:, G.quad, :], lse_tab[bass.ds(b * P, P), :]).then_inc(lblk_in[G.quad], 16)

            def store_agg(G):
                b = scheduled("agg", store_i, G, NB + 4)
                sp.wait_ge(m_agg, G.g + 3)
                sp.dma_start(agg_tab[bass.ds(b * P, P), :], agg_acc[:, G.quad, :]
                             ).then_inc(agg_out[G.quad], 16)

            pipeline(sp, [(load_lse, 8), (store_agg, 0)])
            for k in range(4):
                sp.wait_ge(agg_out[k], 16 * (NG // 4 + 1))
            for k in range(4):
                sp.wait_ge(lblk_in[k], 16 * len(range(k, NG + 8, 4)))

            def load_sums(t, j):
                sp.wait_ge(o_done, t + 1)
                for half, tab in ((0, agg_tab), (1, x)):
                    sp.dma_start(wide_sb[:, j, half * 1024:half * 1024 + LB * D]
                                 .rearrange("p (b c) -> p b c", b=LB),
                                 block_rows(tab, t)).then_inc(o_in[j], 16)

            def store_out(t, j):
                sp.wait_ge(o_done, t + 3)
                sp.dma_start(block_rows(out, t), wide_sb[:, j, 3072:3072 + LB * D]
                             .rearrange("p (b c) -> p b c", b=LB)).then_inc(o_out[j], 16)

            one_ahead(load_sums, store_out)
            for k in range(2):
                sp.wait_ge(o_out[k], 16 * (NB // LB // 2 + 1))

        @block.gpsimd
        def _(pool):
            nc.gpsimd.memset(zeros[:, :], 0.0).then_inc(c_zeros, 1)
            nc.gpsimd.memset(ident[:, :], 0.0).then_inc(c_ident, 1)
            pool.wait_ge(c_ident, 1)
            nc.gpsimd.affine_select(out=ident[:, :], in_=ident[:, :], compare_op=ALU.not_equal,
                                    fill=1.0, base=0, pattern=[[-1, P]],
                                    channel_multiplier=1).then_inc(c_ident, 1)
            nc.gpsimd.iota(first_node_i[:, :], pattern=[[0, 1]], base=0,
                           channel_multiplier=P).then_inc(c_ident, 1)
            nc.gpsimd.iota(iota_gi[:, :], pattern=[[1, NGP]], base=0,
                           channel_multiplier=0).then_inc(c_ident, 1)
            pool.wait_ge(w_in[5], 16)
            pool.indirect_dma_start(rules_sb[:, :], None, rule_emb,
                                    bass.IndirectOffsetOnAxis(ids_sb[:, 0:1], 0)).then_inc(rules_in, 16)
            pool.wait_ge(chunk_ready, 1)
            pool.indirect_dma_start(fine_sb[:, :], None, dst_rows,
                                    bass.IndirectOffsetOnAxis(chunk_i[:, 0:1], 0)).then_inc(fine_in, 16)

            for k in range(2):
                pool.wait_ge(h_out[k], 16 * (1 + len(range(k, NB + 1, 2))))
                pool.wait_ge(x_in[k], 16 * len(range(k, NB + 3, 2)))

            def gather_h(G):
                if G.slot % 2:
                    pool.wait_ge(meta_in[G.slot - 1], G.round * 16)
                    pool.sem_inc(pool_go, 1)
                    pool.wait_ge(meta_in[G.slot], G.round * 16)
                    pool.sem_inc(pool_go, 1)
                    for slot in (G.slot - 1, G.slot):
                        for t in range(TG):
                            pool.indirect_dma_start(
                                rows[:, slot, t, 0:D], None, h_tab,
                                bass.IndirectOffsetOnAxis(meta_sb[:, slot, t, 0:1], 0)
                            ).then_inc(rows_in[slot], 16)

            def decay(G):
                f, part = fmax[:, G.quad, :], diff[:, G.pair, 0:GE]
                pool.wait_ge(s_max, G.g + 1)
                pool.wait_ge(s_exp, G.g + 1)
                nc.gpsimd.tensor_tensor(out=part, in0=f[:, 0:GE], in1=f[:, 1:GE + 1],
                                        op=ALU.subtract).then_inc(s_drop, 1)
                pool.wait_ge(s_drop, G.g + 1)
                nc.gpsimd.tensor_tensor(out=part, in0=part, in1=capT[:, G.pair, :], op=ALU.add
                                        ).then_inc(s_decay, 1)

            pool.sem_inc(s_decay, 2)
            pipeline(pool, [(decay, 3), (gather_h, 9)])

            for k in range(U):
                pool.wait_ge(rows_in[k], 32 * len(range(k, NG + 8, U)))
            for k in range(2):
                pool.wait_ge(proj_out[k], 16 * (NBX + 1))

            def gather_proj(G):
                if G.slot % 4 == 3:
                    pool.wait_ge(m_idx, G.g + 1)
                    pool.sem_inc(pool_go, 1)
                    for slot in range(G.slot - 3, G.slot + 1):
                        for t in range(TG):
                            pool.indirect_dma_start(
                                rows[:, slot, t, 0:D], None, proj_rows,
                                bass.IndirectOffsetOnAxis(idx2[:, slot, t:t + 1], 0)
                            ).then_inc(m_rows_in[slot], 16)
            pipeline(pool, [(gather_proj, 7)])
            for k in range(U):
                pool.wait_ge(m_rows_in[k], 32 * len(range(k, NG + 4, U)))

        @block.scalar
        def _(act):
            act.sem_inc(s_ohT, 1)
            act.sem_inc(s_capT, 1)
            act.sem_inc(s_exp, 2)
            act.sem_inc(s_msT, U)
            act.sem_inc(m_ohT, 1)
            act.sem_inc(m_w, 2)
            act.sem_inc(m_msg, U)
            act.sem_inc(p_copied, 1)
            act.sem_inc(s_maxcarry, 1)
            act.sem_inc(s_sumcarry, 1)
            act.wait_ge(vchain, 2)
            act.wait_ge(w_in[3], 16)

            def deviation(t, j):
                act.wait_ge(n_mv, t + 1)
                nc.scalar.activation(std[:, j, :], mv[:, j, 1:2], ACT.Sqrt, bias=eps[:, :]
                                     ).then_inc(n_std, 1)

            def copy_hT(t, j):
                act.wait_ge(n_hTp, t + 1)
                nc.scalar.activation(hTs[:, bass.ds(t * P, P)], bank[0 + j][:, 0:P], ACT.Copy
                                     ).then_inc(n_hT, 1)
                act.wait_ge(n_hT, t + 1)
                nc.scalar.activation(hT2[:, j, :], bank[0 + j][:, 0:P], ACT.Copy).then_inc(n_hT2, 1)

            def copy_qT(t, j):
                act.wait_ge(n_qTp, t + 1)
                nc.scalar.activation(qT[:, j, :], bank[2 + j][:, 0:P], ACT.Identity,
                                     bias=wqb_sb[:, :]).then_inc(n_qT, 1)

            deviation(0, 0)
            deviation(1, 1)
            with act.Fori(0, NB // NODES) as i:
                for j in range(NODES):
                    copy_hT(i * NODES + j, j % 2)
                    deviation(i * NODES + (j + 2), j % 2)
                    copy_qT(i * NODES + j, j % 2)

            def operand(i):
                nc.scalar.activation(hT[:, :], hTs[:, bass.ds(i * P, P)], ACT.Copy).then_inc(p_hT, 1)

            act.wait_ge(n_hT, 1)
            operand(0)

            def proj_copies(i, j):
                if j % (U // 2) == 0:
                    act.wait_ge(proj_out[j // (U // 2)], (i + 1) * 16)
                act.wait_ge(p_prod, i * U + (j + 1))
                c = j % (U // 2)
                nc.scalar.activation(proj[:, j // (U // 2), c * 512:(c + 1) * 512], bank[4][:, :],
                                     ACT.Copy).then_inc(p_copied, 1)
                if j == U - 1:
                    operand(i + 1)
                if j % (U // 2) == U // 2 - 1:
                    half = j // (U // 2)
                    act.wait_ge(p_copied, i * U + (j + 2))
                    act.dma_start(proj_tab[bass.ds(i * P, P), half * 2048:(half + 1) * 2048],
                                  proj[:, half, :]).then_inc(proj_out[half], 16)

            def copy_ohT(G):
                act.wait_ge(s_ohTp, G.g + 1)
                act.wait_ge(s_qexp, G.g + 1)
                nc.scalar.activation(ohT[:, G.pair, :], bank[0][:, 0:GE], ACT.Copy).then_inc(s_ohT, 1)

            def copy_capT(G):
                act.wait_ge(s_capTp, G.g + 1 + U)
                act.wait_ge(s_decay, G.g + 1)
                nc.scalar.activation(capT[:, G.pair, :],
                                     bank[5][:, :].bitcast(mybir.dt.bfloat16)[:, 0:GE],
                                     ACT.Copy).then_inc(s_capT, 1)

            def edge_relation(G):
                act.wait_ge(meta_in[G.slot], G.round * 16)
                nc.scalar.activation(ets[:, bass.ds(G.g * TG, TG)], meta_sb[:, G.slot, :, 1], ACT.Copy
                                     ).then_inc(s_et, 1)

            def carry_max(G):
                act.wait_ge(s_max, G.g + 1)
                nc.scalar.activation(fmax[:, G.next_quad, 0:1], fmax[:, G.quad, GE:GE + 1], ACT.Copy
                                     ).then_inc(s_maxcarry, 1)

            def carry_sum(G):
                act.wait_ge(s_sum, G.g + 3)
                nc.scalar.activation(ssum[:, 1 - G.pair, 0:1], ssum[:, G.pair, GE:GE + 1], ACT.Copy
                                     ).then_inc(s_sumcarry, 1)

            def exponentials(G):
                act.wait_ge(s_diff, G.g + 3)
                act.wait_ge(s_decay, G.g + 3)
                act.wait_ge(s_sum, G.g + 1)
                nc.scalar.activation(expd[:, G.pair, :], diff[:, G.pair, :], ACT.Exp).then_inc(s_exp, 1)

            def keep_last(G):
                act.wait_ge(s_msTp, G.g + 5)
                act.wait_ge(s_msp, G.g + U - 1)
                for t in range(TG):
                    done = nc.scalar.activation(ms_last[:, G.pair, t, :],
                                                bank[6][:, t * 256:(t + 1) * 256], ACT.Copy,
                                                scale=ends[:, G.slot, t, 1:2])
                done.then_inc(s_msT, 1)

            pipeline(act, [(exponentials, 2), (copy_ohT, 6), (carry_max, 3), (keep_last, 1),
                           (edge_relation, 7), (copy_capT, 4), (carry_sum, 2)], proj_copies, 4)

            with act.Fori(0, NB // LB // 2) as i:
                for j in range(2):
                    t = i * 2 + j
                    act.wait_ge(l_pos, t + 1)
                    nc.scalar.activation(wide_sb[:, j, 2048:2048 + LB * A * R],
                                         wide_sb[:, j, 2048:2048 + LB * A * R], ACT.Ln).then_inc(l_ln, 1)

            def copy_idx(G):
                nc.scalar.activation(idx2[:, G.slot, :], idx2s[:, bass.ds(G.g * TG, TG)],
                                     ACT.Copy).then_inc(m_idx, 1)

            def copy_moh(G):
                act.wait_ge(m_ohTp, G.g + 1)
                act.wait_ge(m_lexp, G.g + 3)
                nc.scalar.activation(ohT[:, G.pair, :], bank[0][:, 0:GE], ACT.Copy).then_inc(m_ohT, 1)

            def weights(G):
                act.wait_ge(m_z, G.g + 1)
                for t in range(TG):
                    done = nc.scalar.activation(ez[:, G.pair, t, :], z[:, G.pair, t, :], ACT.Exp,
                                                accum_out=wsum[:, G.pair, t:t + 1])
                done.then_inc(m_w, 1)

            def messages(G):
                act.wait_ge(m_rows_in[G.slot], G.round * 32)
                act.wait_ge(m_aggp, G.g + U - 1)
                act.wait_ge(m_w, G.g + 3)
                for t in range(TG):
                    done = nc.scalar.activation(msg[:, G.pair, t, :], rows[:, G.slot, t, 0:D],
                                                ACT.Copy, scale=wsum[:, G.pair, t:t + 1])
                done.then_inc(m_msg, 1)

            pipeline(act, [(copy_moh, 4), (weights, 2), (messages, 2), (copy_idx, 10)])

            with act.Fori(0, NB // LB // 2) as i:
                for j in range(2):
                    t = i * 2 + j
                    act.wait_ge(o_mv, t + 1)
                    nc.scalar.activation(ostd[:, j, :], omv[:, j, :, 1], ACT.Sqrt, bias=eps[:, :]
                                         ).then_inc(o_std, 1)

        @block.tensor
        def _(pe):
            pe.sem_inc(s_qexp, 2)
            pe.sem_inc(s_capTp, U)
            pe.sem_inc(s_msTp, 4)
            pe.sem_inc(s_msTp2, 2)
            pe.sem_inc(s_msp, U)
            pe.sem_inc(m_lexp, 4)
            pe.sem_inc(m_aggp, U)
            pe.wait_ge(c_ident, 4)
            pe.wait_ge(rules_in, 16)
            nc.tensor.transpose(bank[6][:, 0:A], rules_sb[:, :], ident[0:A, 0:A]).then_inc(rulesTp, 1)
            pe.wait_ge(start_ready, 1)
            nc.tensor.matmul(bank[0][:, 0:P], start_col[:, 0:1].to_broadcast([P, P]), ident[:, :],
                             start=True, stop=True).then_inc(startT, 1)
            pe.wait_ge(gend_ready, 2)
            nc.tensor.transpose(bank[1][0:NB, 0:P], gend[:, 0:NB], ident[:, :])
            nc.tensor.transpose(bank[1][0:NB, P:2 * P], kstep[:, 0:NB], ident[:, :]).then_inc(gendT, 1)
            pe.wait_ge(passed_ready, 1)
            for c in range(2):
                part = slice(c * NGP // 2, (c + 1) * NGP // 2)
                nc.tensor.matmul(bank[2 + c][:, 0:NGP // 2], ones[0:NB, :], passed[0:NB, part],
                                 start=True, stop=True)
                done = nc.tensor.matmul(bank[4 + c][0:1, 0:NGP // 2], kstep_col[0:NB, :],
                                        passed[0:NB, part], start=True, stop=True)
            done.then_inc(blkp, 1)
            pe.wait_ge(w_in[2], 16)
            nc.tensor.transpose(bank[7][:, 0:D], wk_sb[:, 0, :], ident[:, :])
            pe.wait_ge(rulesT, 2)
            nc.tensor.matmul(bank[7][:, D:D + R], wk_sb[:, 1, :], hrelT_sb[:, :], start=True, stop=True)
            nc.tensor.matmul(bank[7][:, D + R:QW], wk_sb[:, 2, :], rulesT_sb[:, :], start=True,
                             stop=True).then_inc(qwp, 1)
            pe.wait_ge(qw_ready, 1)
            pe.wait_ge(sched_ready, 1)
            pe.wait_ge(w_in[0], 16)
            pe.wait_ge(w_in[1], 16)

            def transpose_h(t, j):
                pe.wait_ge(n_h, t + 1)
                nc.tensor.transpose(bank[0 + j][:, 0:P], h[:, j, :], ident[:, :]).then_inc(n_hTp, 1)

            def node_q(t, j):
                pe.wait_ge(n_hT2, t + 1)
                nc.tensor.matmul(bank[2 + j][:, 0:P], wq_sb[:, :], hT2[:, j, :], start=True,
                                 stop=True).then_inc(n_qTp, 1)

            def node_qt(t, j):
                pe.wait_ge(n_qT, t + 1)
                nc.tensor.matmul(bank[4 + j][:, 0:QW], qT[:, j, :], qw_sb[:, :], start=True,
                                 stop=True).then_inc(n_qtp, 1)

            transpose_h(0, 0)
            with pe.Fori(0, NB // NODES) as i:
                for j in range(NODES):
                    node_q(i * NODES + j, j % 2)
                    transpose_h(i * NODES + (j + 1), (j + 1) % 2)
                    node_qt(i * NODES + j, j % 2)
            pe.wait_ge(n_qt, NB)
            pe.wait_ge(n_hT, NB)

            def proj_product(i, j):
                if j == 0:
                    pe.wait_ge(p_hT, i + 1)
                pe.wait_ge(p_copied, i * U + (j + 1))
                nc.tensor.matmul(bank[4][:, :], hT[:, :], w_sb[:, j * 512:(j + 1) * 512],
                                        start=True, stop=True).then_inc(p_prod, 1)

            def transpose_onehot(G):
                pe.wait_ge(s_prep, G.g + 1 + U)
                pe.wait_ge(s_ohT, G.g + 1)
                for t in range(TG):
                    done = nc.tensor.transpose(bank[0][:, t * P:(t + 1) * P], onehot[:, G.slot, t, :],
                                               ident[:, :])
                done.then_inc(s_ohTp, 1)

            def expand_q(G):
                pe.wait_ge(s_ohT, G.g + 2)
                pe.wait_ge(qblk_in[G.pair], G.pround * 16)
                pe.wait_ge(s_x4, G.g + 1)
                for t in range(TG):
                    done = nc.tensor.matmul(bank[1 + G.pair][:, t * 256:t * 256 + QW],
                                            ohT[:, G.pair, t * P:(t + 1) * P], qblk[:, G.pair, :],
                                            start=True, stop=True)
                done.then_inc(s_qexp, 1)

            def transpose_masked(G):
                pe.wait_ge(s_mask, G.g + 1 + U)
                pe.wait_ge(s_diff, G.g + 2)
                for t in range(TG):
                    done = nc.tensor.transpose(bank[3][:, t * P:(t + 1) * P], masked[:, G.pair, t, :],
                                               ident[:, :])
                done.then_inc(s_maskT, 1)
                pe.wait_ge(s_capT, G.g + 1)
                for t in range(TG):
                    done = nc.tensor.transpose(
                        bank[5][:, :].bitcast(mybir.dt.bfloat16)[:, t * P:(t + 1) * P],
                        capnew[:, G.slot, t:t + 1].to_broadcast([P, P]), ident_b[:, :])
                done.then_inc(s_capTp, 1)

            def transpose_ms(G):
                pe.wait_ge(s_sum, G.g + 3)
                pe.wait_ge(s_msT, G.g + U)
                for t in range(TG):
                    for q, source in enumerate((fmax[:, G.quad, :], ssum[:, G.pair, :])):
                        done = nc.tensor.transpose(
                            bank[6][:, t * 256 + q * P:t * 256 + (q + 1) * P],
                            source[:, 1 + t * P:1 + (t + 1) * P], ident[:, :])
                done.then_inc(s_msTp, 1)
                pe.sem_inc(s_msTp2, 1)

            def place_ms(G):
                pe.wait_ge(s_msT, G.g + 1 + U)
                pe.wait_ge(s_ms, G.g + 1)
                for t in range(TG):
                    done = nc.tensor.matmul(bank[7][:, 0:2 * A * R], onehot[:, G.slot, t, :],
                                            ms_last[:, G.pair, t, :], start=(t == 0), stop=(t == TG - 1))
                done.then_inc(s_msp, 1)

            pipeline(pe, [(transpose_onehot, 6), (transpose_ms, 1), (place_ms, 0),
                          (expand_q, 6), (transpose_masked, 4)], proj_product, 3)

            def transpose_moh(G):
                pe.wait_ge(m_oh, G.g + 1)
                pe.wait_ge(m_ohT, G.g + 1)
                for t in range(TG):
                    done = nc.tensor.transpose(bank[0][:, t * P:(t + 1) * P], onehot[:, G.slot, t, :],
                                               ident[:, :])
                done.then_inc(m_ohTp, 1)

            def expand_lse(G):
                pe.wait_ge(m_ohT, G.g + 2)
                pe.wait_ge(lblk_in[G.quad], G.qround * 16)
                pe.wait_ge(m_pick, G.g + U - 1)
                for t in range(TG):
                    done = nc.tensor.matmul(bank[1 + G.pair][:, t * P:(t + 1) * P],
                                            ohT[:, G.pair, t * P:(t + 1) * P], lblk[:, G.quad, :],
                                            start=True, stop=True)
                done.then_inc(m_lexp, 1)

            def aggregate(G):
                pe.wait_ge(m_msg, G.g + 1 + U)
                pe.wait_ge(m_agg, G.g + 1)
                for t in range(TG):
                    done = nc.tensor.matmul(bank[3 + G.pair][:, 0:D], onehot[:, G.slot, t, :],
                                            msg[:, G.pair, t, :], start=(t == 0), stop=(t == TG - 1))
                done.then_inc(m_aggp, 1)

            pipeline(pe, [(transpose_moh, 4), (aggregate, 1), (expand_lse, 4)])

        @block.vector
        def _(dve):
            steps = [0]

            def chain(ins):
                steps[0] += 1
                ins.then_inc(vchain, 1)
                dve.wait_ge(vchain, steps[0])

            V = nc.vector
            chain(V.memset(ones[:, :], 1.0))
            chain(V.memset(eps[:, :], EPS))
            dve.sem_inc(n_hc, 2)
            dve.sem_inc(s_prep, U)
            dve.sem_inc(s_dot, U)
            dve.sem_inc(s_x4, 2)
            dve.sem_inc(s_mask, U)
            dve.sem_inc(s_diff, 2)
            dve.sem_inc(s_sum, 2)
            dve.sem_inc(s_ms, 1)
            dve.sem_inc(l_sum, 2)
            dve.sem_inc(m_pick, U)
            dve.sem_inc(o_done, 2)
            dve.wait_ge(c_ident, 4)
            chain(V.tensor_copy(first_node[:, :], first_node_i[:, :]))
            chain(V.tensor_copy(iota_g[:, :], iota_gi[:, :]))
            chain(V.tensor_copy(iota[:, :], iota_gi[:, 0:P]))
            chain(V.tensor_copy(ident_b[:, :], ident[:, :]))

            dve.wait_ge(w_in[9], 16)
            chain(V.tensor_copy(samp_f[:, 0:NSAMP], samp_sb[:, :]))
            chain(V.tensor_scalar(below[:, 0:NSAMP], samp_f[:, 0:NSAMP], first_node[:, :], None,
                                  ALU.is_lt, ALU.add, accum_out=coarse[:, :]))
            chain(V.tensor_scalar(chunk[:, :], coarse[:, :], -1.0, 0.0, ALU.add, ALU.max))
            V.tensor_copy(chunk_i[:, :], chunk[:, :]).then_inc(chunk_ready, 1)
            dve.wait_ge(fine_in, 16)
            chain(V.tensor_copy(samp_f[:, :], fine_sb[:, :]))
            chain(V.tensor_scalar(below[:, :], samp_f[:, :], first_node[:, :], None,
                                  ALU.is_lt, ALU.add, accum_out=fine[:, :]))
            V.scalar_tensor_tensor(out=start_col[:, :], in0=chunk[:, :], scalar=float(SAMPLE),
                                   in1=fine[:, :], op0=ALU.mult, op1=ALU.add).then_inc(start_ready, 1)
            dve.wait_ge(startT, 1)
            chain(V.tensor_copy(start_row[:, :], bank[0][:, 0:P]))
            chain(V.scalar_tensor_tensor(out=cnt_i[:, :], in0=start_row[:, 1:NB + 1],
                                         scalar=float(GE - 1), in1=start_row[:, 0:NB],
                                         op0=ALU.add, op1=ALU.subtract))
            chain(V.tensor_scalar(groups_i[:, :], cnt_i[:, :], GE.bit_length() - 1, None,
                                  ALU.arith_shift_right))
            chain(V.tensor_copy(groups[:, 0:NB], groups_i[:, :]))
            V.tensor_tensor_scan(gend[:, 0:NB], ones[:, 0:NB], groups[:, 0:NB], 0.0, ALU.mult,
                                 ALU.add).then_inc(gend_ready, 1)
            dve.wait_ge(gend_ready, 1)
            chain(V.tensor_tensor(out=groups[:, 0:NB], in0=gend[:, 0:NB], in1=groups[:, 0:NB],
                                  op=ALU.subtract))
            chain(V.scalar_tensor_tensor(out=kshift[:, 0:NB], in0=groups[:, 0:NB],
                                         scalar=-float(GE), in1=start_row[:, 0:NB], op0=ALU.mult,
                                         op1=ALU.add))
            chain(V.scalar_tensor_tensor(out=kshift[:, NB:NB + 1], in0=gend[:, NB - 1:NB],
                                         scalar=-float(GE), in1=start_row[:, NB:NB + 1],
                                         op0=ALU.mult, op1=ALU.add))
            V.tensor_tensor(out=kstep[:, 0:NB], in0=kshift[:, 1:NB + 1], in1=kshift[:, 0:NB],
                            op=ALU.subtract).then_inc(gend_ready, 1)
            dve.wait_ge(gendT, 1)
            chain(V.tensor_copy(gend_col[0:NB, :], bank[1][0:NB, 0:1]))
            chain(V.tensor_copy(kstep_col[0:NB, :], bank[1][0:NB, P:P + 1]))
            V.tensor_scalar(passed[0:NB, :], iota_g[0:NB, :], gend_col[0:NB, :], None,
                            ALU.is_ge).then_inc(passed_ready, 1)
            dve.wait_ge(blkp, 1)
            for c in range(2):
                part = slice(c * NGP // 2, (c + 1) * NGP // 2)
                chain(V.tensor_copy(blk[:, part], bank[2 + c][:, 0:NGP // 2]))
                chain(V.scalar_tensor_tensor(out=e0f[:, part], in0=iota_g[0:1, part],
                                             scalar=float(GE), in1=bank[4 + c][0:1, 0:NGP // 2],
                                             op0=ALU.mult, op1=ALU.add))
            chain(V.tensor_scalar(e0_i[:, :], e0f[:, :], float(E), None, ALU.min))
            chain(V.tensor_copy(blk_i[:, :], blk[0:1, :]))
            chain(V.tensor_scalar(blk128[:, :], blk[:, :], float(P), None, ALU.mult))
            chain(V.memset(keep[:, 0:1], 0.0))
            chain(V.tensor_tensor(out=keep[:, 1:NGP], in0=blk[:, 1:NGP], in1=blk[:, 0:NGP - 1],
                                  op=ALU.is_equal))
            chain(V.memset(e0f[:, NGP - 1:NGP], 0.0))
            for k in range(4):
                chain(V.tensor_scalar(e0f[:, k:NGP - 1:4], blk[0:1, k:NGP - 1:4], -1.0,
                                      float(NB + 1 + k), ALU.mult, ALU.add))
            chain(V.tensor_tensor(out=e0f[:, 0:NGP - 1], in0=e0f[:, 0:NGP - 1],
                                  in1=keep[0:1, 1:NGP], op=ALU.mult))
            V.tensor_tensor(out=store_i[:, :], in0=e0f[:, :], in1=blk[0:1, :],
                            op=ALU.add).then_inc(sched_ready, 1)

            dve.wait_ge(rulesTp, 1)
            V.tensor_copy(rulesT_sb[:, :], bank[6][:, 0:A]).then_inc(rulesT, 1)
            dve.wait_ge(w_in[0], 16)
            chain(V.tensor_reduce(hrelT_sb[:, :], w_sb[:, :].rearrange("d (r o) -> d r o", r=R),
                                  AX.X, ALU.add))
            V.tensor_scalar(hrelT_sb[:, :], hrelT_sb[:, :], 1.0 / D, None, ALU.mult).then_inc(rulesT, 1)
            dve.wait_ge(qwp, 1)
            dve.wait_ge(w_in[4], 16)
            chain(V.tensor_copy(qw_sb[:, :], bank[7][:, 0:QW]))
            chain(V.tensor_scalar(qw_sb[:, D:D + R], qw_sb[:, D:D + R], wkb_sb[:, :], None, ALU.add))
            V.tensor_scalar(qw_sb[:, :], qw_sb[:, :], SCALE, None, ALU.mult).then_inc(qw_ready, 1)
            chain(V.memset(idx2s[:, NG * TG:], 0))
            chain(V.memset(fmax[:, 0, 0:1], -BIG))
            chain(V.memset(ssum[:, 0, 0:1], 0.0))
            chain(V.memset(hTs[:, NP:(NBX + 1) * P], 0.0))
            chain(V.memset(ms_acc[:, :, :], 0.0))

            def normalize(t, j, rnd):
                dve.wait_ge(x_in[j], rnd * 16)
                V.bn_stats(stats[:, j, :], xt[:, j, :]).then_inc(n_stats, 1)
                dve.wait_ge(n_stats, t + 1)
                dve.sem_inc(n_seen, 1)
                V.bn_aggr(mv[:, j, :], stats[:, j, :]).then_inc(n_mv, 1)
                dve.wait_ge(n_std, t + 1)
                V.reciprocal(rstd[:, j, :], std[:, j, :]).then_inc(n_rstd, 1)
                dve.wait_ge(n_rstd, t + 1)
                V.tensor_scalar(hc[:, j, :], xt[:, j, :], mv[:, j, 0:1], rstd[:, j, :],
                                ALU.subtract, ALU.mult).then_inc(n_hc, 1)
                dve.wait_ge(n_hc, t + 3)
                dve.wait_ge(h_out[j], rnd * 16)
                V.tensor_scalar(h[:, j, :], hc[:, j, :], 0.0, None, ALU.max).then_inc(n_h, 1)

            def node_evacuate(t, j, rnd):
                dve.wait_ge(n_qtp, t + 1)
                dve.wait_ge(qt_out[j], rnd * 16)
                V.tensor_copy(qt[:, j, :], bank[4 + j][:, 0:QW]).then_inc(n_qt, 1)

            normalize(0, 0, 1)
            normalize(1, 1, 1)
            with dve.Fori(0, NB // NODES) as i:
                for j in range(NODES):
                    rnd = i * (NODES // 2)
                    normalize(i * NODES + (j + 2), j % 2, rnd + (j // 2 + 2))
                    node_evacuate(i * NODES + j, j % 2, rnd + (j // 2 + 1))

            for k in range(2):
                dve.wait_ge(h_out[k], 16 * (1 + len(range(k, NB + 1, 2))))
                dve.wait_ge(x_in[k], 16 * len(range(k, NB + 3, 2)))

            def edge_fields(G):
                edge = meta_sb[:, G.slot, :, :]
                dve.wait_ge(meta_in[G.slot], G.round * 16)
                V.tensor_tensor(out=dlocs[:, bass.ds(G.g * TG, TG)], in0=edge[:, :, 3],
                                in1=blk128[:, bass.ds(G.g, 1)].to_broadcast([P, TG]),
                                op=ALU.subtract).then_inc(s_dloc, 1)
                V.scalar_tensor_tensor(out=idx2s[:, bass.ds(G.g * TG, TG)], in0=edge[:, :, 0],
                                       scalar=float(R), in1=edge[:, :, 1], op0=ALU.mult, op1=ALU.add)
                dve.wait_ge(s_msT, G.g + 1)
                V.tensor_tensor(out=ends[:, G.slot, :, :], in0=edge[:, :, 2:5:2],
                                in1=edge[:, :, 3:4].to_broadcast([P, TG, 2]),
                                op=ALU.not_equal).then_inc(s_isnew, 1)
                dve.wait_ge(s_dot, G.g + 1)
                V.tensor_tensor(out=rows[:, G.slot, :, D:D + R],
                                in0=iota[:, None, 0:R].to_broadcast([P, TG, R]),
                                in1=edge[:, :, 1:2].to_broadcast([P, TG, R]),
                                op=ALU.is_equal).then_inc(s_ohr, 1)

            def edge_masks(G):
                dve.wait_ge(s_dloc, G.g + 1)
                dve.wait_ge(s_msp, G.g + 1)
                V.tensor_tensor(out=onehot[:, G.slot, :, :],
                                in0=iota[:, None, 0:P].to_broadcast([P, TG, P]),
                                in1=dlocs[:, bass.ds(G.g * TG, TG), None].to_broadcast([P, TG, P]),
                                op=ALU.is_equal)
                dve.wait_ge(s_isnew, G.g + 1)
                dve.wait_ge(s_capTp, G.g + 1)
                V.tensor_scalar(capnew[:, G.slot, :], ends[:, G.slot, :, 0], -BIG, None, ALU.mult)
                dve.wait_ge(s_ohr, G.g + 1)
                dve.wait_ge(s_mask, G.g + 1)
                V.tensor_scalar(caprel[:, G.slot, :, :], rows[:, G.slot, :, D:D + R], 2 * BIG, -BIG,
                                ALU.mult, ALU.add).then_inc(s_prep, 1)

            def score_dots(G):
                dve.wait_ge(rows_in[G.slot], G.round * 32)
                dve.wait_ge(s_qexp, G.g + 3)
                for t in range(TG):
                    done = V.tensor_tensor_reduce(
                        out=prod[:, G.pair, t, :], in0=bank[1 + G.pair][:, t * 256:t * 256 + D + R],
                        in1=rows[:, G.slot, t, :], scale=1.0, scalar=0.0, op0=ALU.mult, op1=ALU.add,
                        accum_out=dots[:, G.pair, t:t + 1])
                done.then_inc(s_dot, 1)

            def score_rules(G):
                q = bank[1 + G.pair][:, :].rearrange("p (t c) -> p t c", t=TG)
                dve.wait_ge(s_dot, G.g + 1 + U)
                V.tensor_tensor(out=scores[:, bass.ds(G.g * TG, TG), :], in0=q[:, :, D + R:QW],
                                in1=dots[:, G.pair, :, None].to_broadcast([P, TG, A]),
                                op=ALU.add).then_inc(s_x4, 1)

            def score_lanes(G):
                dve.wait_ge(s_x4, G.g + 3)
                dve.wait_ge(s_prep, G.g + 1 + U)
                V.tensor_tensor(
                    out=masked[:, G.pair, :, :].rearrange("p t (a r) -> p t a r", a=A),
                    in0=scores[:, bass.ds(G.g * TG, TG), :, None].to_broadcast([P, TG, A, R]),
                    in1=caprel[:, G.slot, :, None, :].to_broadcast([P, TG, A, R]),
                    op=ALU.min).then_inc(s_mask, 1)

            def running_max(G):
                f, cap, lanes = fmax[:, G.quad, :], capT[:, G.pair, :], bank[3][:, 0:GE]
                dve.wait_ge(s_maskT, G.g + 1)
                dve.wait_ge(s_capT, G.g + 2)
                dve.wait_ge(s_msTp, G.g + 1)
                dve.wait_ge(s_maxcarry, G.g + 1)
                V.tensor_tensor_scan(f[:, 1:GE + 1], cap, lanes, f[:, 0:1], ALU.add,
                                     ALU.max).then_inc(s_max, 1)

            def score_excess(G):
                dve.wait_ge(s_max, G.g + 1)
                dve.wait_ge(s_exp, G.g + 1)
                V.tensor_tensor(out=diff[:, G.pair, GE:2 * GE], in0=bank[3][:, 0:GE],
                                in1=fmax[:, G.quad, 1:GE + 1], op=ALU.subtract).then_inc(s_diff, 1)

            def running_sum(G):
                dve.wait_ge(s_exp, G.g + 3)
                dve.wait_ge(s_msTp2, G.g + 1)
                dve.wait_ge(s_sumcarry, G.g + 1)
                V.tensor_tensor_scan(ssum[:, G.pair, 1:GE + 1], expd[:, G.pair, 0:GE],
                                     expd[:, G.pair, GE:2 * GE], ssum[:, G.pair, 0:1], ALU.mult,
                                     ALU.add).then_inc(s_sum, 1)

            def accumulate_ms(G):
                dve.wait_ge(s_msp, G.g + 1 + U)
                dve.wait_ge(ms_out, (G.g + 1) * 16)
                dve.wait_ge(s_ms, G.g + 1)
                V.scalar_tensor_tensor(out=ms_acc[:, G.pair, :], in0=ms_acc[:, 1 - G.pair, :],
                                       scalar=keep[:, bass.ds(G.g, 1)], in1=bank[7][:, 0:2 * A * R],
                                       op0=ALU.mult, op1=ALU.add).then_inc(s_ms, 1)

            pipeline(dve, [(running_max, 3), (edge_fields, 7), (score_excess, 3), (edge_masks, 7),
                           (score_dots, 5), (accumulate_ms, 0), (score_rules, 5), (running_sum, 2),
                           (score_lanes, 5)])

            with dve.Fori(0, NB // LB // 2) as i:
                for j in range(2):
                    t = i * 2 + j
                    ms = wide_sb[:, j, 0:LB * 2 * A * R].rearrange("p (b c) -> p b c", b=LB)
                    tmp = wide_sb[:, j, 2048:2048 + LB * A * R].rearrange("p (b c) -> p b c", b=LB)
                    dve.wait_ge(l_in[j], (i + 1) * 16)
                    V.tensor_scalar(tmp, ms[:, :, A * R:], 1e-30, None, ALU.max).then_inc(l_pos, 1)
                    dve.wait_ge(l_ln, t + 1)
                    dve.wait_ge(l_out[j], (i + 1) * 16)
                    V.tensor_tensor(out=wide_sb[:, j, 3072:3072 + LB * A * R]
                                    .rearrange("p (b c) -> p b c", b=LB),
                                    in0=ms[:, :, 0:A * R], in1=tmp, op=ALU.add).then_inc(l_sum, 1)

            def message_masks(G):
                dve.wait_ge(m_pick, G.g + 1)
                V.tensor_tensor(out=rows[:, G.slot, :, D:D + R],
                                in0=iota[:, None, 0:R].to_broadcast([P, TG, R]),
                                in1=ets[:, bass.ds(G.g * TG, TG), None].to_broadcast([P, TG, R]),
                                op=ALU.is_equal)
                dve.wait_ge(m_aggp, G.g + 1)
                V.tensor_tensor(out=onehot[:, G.slot, :, :],
                                in0=iota[:, None, 0:P].to_broadcast([P, TG, P]),
                                in1=dlocs[:, bass.ds(G.g * TG, TG), None].to_broadcast([P, TG, P]),
                                op=ALU.is_equal).then_inc(m_oh, 1)

            def exponents(G):
                dve.wait_ge(m_lexp, G.g + 5)
                dve.wait_ge(m_oh, G.g + 1)
                dve.wait_ge(m_lse, G.g + 1)
                V.tensor_tensor(out=picked[:, G.pair, :, :, :],
                                in0=bank[1 + G.pair][:, 0:GE].rearrange("p (t a r) -> p t a r", t=TG, a=A),
                                in1=rows[:, G.slot, :, None, D:D + R].to_broadcast([P, TG, A, R]),
                                op=ALU.mult).then_inc(m_pick, 1)
                dve.wait_ge(m_pick, G.g + 1 + U)
                V.tensor_reduce(lse[:, G.pair, :, :], picked[:, G.pair, :, :, :], AX.X, ALU.add
                                ).then_inc(m_lse, 1)
                dve.wait_ge(m_lse, G.g + 2)
                dve.wait_ge(m_w, G.g + 1)
                V.tensor_tensor(out=z[:, G.pair, :, :], in0=scores[:, bass.ds(G.g * TG, TG), :],
                                in1=lse[:, G.pair, :, :], op=ALU.subtract).then_inc(m_z, 1)

            def accumulate_agg(G):
                dve.wait_ge(m_aggp, G.g + 1 + U)
                dve.wait_ge(agg_out[G.quad], G.qround * 16)
                dve.wait_ge(m_agg, G.g + 2)
                V.scalar_tensor_tensor(out=agg_acc[:, G.quad, :], in0=agg_acc[:, (G.quad + 3) % 4, :],
                                       scalar=keep[:, bass.ds(G.g, 1)], in1=bank[3 + G.pair][:, 0:D],
                                       op0=ALU.mult, op1=ALU.add).then_inc(m_agg, 1)

            dve.wait_ge(p_hT, NBX + 1)
            V.memset(agg_acc[:, :, :], 0.0).then_inc(m_agg, 2)
            dve.sem_inc(m_lse, 1)
            pipeline(dve, [(exponents, 3), (message_masks, 5), (accumulate_agg, 0)])

            base = steps[0]
            OSTEPS = 7
            with dve.Fori(0, NB // LB // 2) as i:
                for j in range(2):
                    t = i * 2 + j
                    n = [0]

                    def ochain(ins):
                        n[0] += 1
                        ins.then_inc(vchain, 1)
                        dve.wait_ge(vchain, t * OSTEPS + (base + n[0]))

                    def wide(v):
                        return v.rearrange("p (b c) -> p b c", b=LB)
                    agg = wide(wide_sb[:, j, 0:LB * D])
                    res = wide(wide_sb[:, j, 1024:1024 + LB * D])
                    y = wide(wide_sb[:, j, 2048:2048 + LB * D])
                    o = wide(wide_sb[:, j, 3072:3072 + LB * D])
                    full = [P, LB, D]
                    dve.wait_ge(o_in[j], (i + 1) * 32)
                    ochain(V.scalar_tensor_tensor(out=y, in0=agg, scalar=1.0 / A,
                                                  in1=bias_sb[:, None, :].to_broadcast(full),
                                                  op0=ALU.mult, op1=ALU.add))
                    for b in range(LB):
                        done = V.bn_stats(ostats[:, j, b, :], y[:, b, :])
                    ochain(done)
                    dve.sem_inc(n_seen, 1)
                    for b in range(LB):
                        done = V.bn_aggr(omv[:, j, b, :], ostats[:, j, b, :])
                    done.then_inc(o_mv, 1)
                    dve.wait_ge(o_mv, t + 1)
                    dve.wait_ge(o_std, t + 1)
                    V.reciprocal(orstd[:, j, :], ostd[:, j, :])
                    ochain(V.tensor_tensor(out=y, in0=y, in1=omv[:, j, :, 0:1].to_broadcast(full),
                                           op=ALU.subtract))
                    ochain(V.tensor_tensor(out=y, in0=y, in1=orstd[:, j, :, None].to_broadcast(full),
                                           op=ALU.mult))
                    ochain(V.tensor_tensor(out=y, in0=y, in1=gamma_sb[:, None, :].to_broadcast(full),
                                           op=ALU.mult))
                    ochain(V.tensor_tensor(out=y, in0=y, in1=beta_sb[:, None, :].to_broadcast(full),
                                           op=ALU.add))
                    dve.wait_ge(o_out[j], (i + 1) * 16)
                    ochain(V.scalar_tensor_tensor(out=o, in0=y, scalar=0.0, in1=res, op0=ALU.max,
                                                  op1=ALU.add))
                    dve.sem_inc(o_done, 1)


def kernel(**inputs):
    import numpy as np
    import concourse.bacc as bacc
    from concourse.bass_utils import run_bass_kernel_spmd

    x = np.ascontiguousarray(inputs["x"])
    xpad = np.zeros(((NB + 3) * P, D), x.dtype)
    xpad[:N] = x
    src, dst, et = (np.ascontiguousarray(inputs[k]) for k in ("src", "dst", "edge_type_32"))
    meta = np.zeros((E + GE, 5), src.dtype)
    meta[:, 2:5] = PAD_DST
    meta[:E, 0] = src
    meta[:E, 1] = et
    meta[:E, 3] = dst
    meta[0, 2] = -1
    meta[1:E + 1, 2] = dst
    meta[:E - 1, 4] = dst[1:]
    rows = np.full((NSAMP, SAMPLE), PAD_DST, dst.dtype)
    rows.reshape(-1)[:E] = dst
    arrays = {"x": xpad, "meta": meta, "samples": np.ascontiguousarray(rows[:, 0]), "dst_rows": rows}
    for name in ("W_r", "Wq_w", "Wq_b", "Wk_w", "Wk_b", "rule_emb", "rule_ids", "bias", "ln_gamma",
                 "ln_beta"):
        arrays[name] = np.ascontiguousarray(inputs["L0_gnn_" + name])

    nc = bacc.Bacc("TRN2", target_bir_lowering=False, num_devices=1)
    args = [nc.dram_tensor("in_" + n, a.shape, mybir.dt.from_np(a.dtype), kind="ExternalInput").ap()
            for n, a in arrays.items()]
    out = nc.dram_tensor("out_0", (NP, D), mybir.dt.float32, kind="ExternalOutput").ap()
    build(nc, *args, out)
    r = run_bass_kernel_spmd(nc, [{"in_" + n: a for n, a in arrays.items()}], core_ids=[0])
    return r.results[0]["out_0"][:N]
```
